# Optimizing a Trainium2 kernel written in Bass

```python
import numpy as np
import jax
import jax.numpy as jnp

def _softmax(x, axis=-1):
    return jax.nn.softmax(x, axis=axis)

def _gelu(x):
    return jax.nn.gelu(x, approximate=True)

def _silu(x):
    return jax.nn.silu(x)

def _sigmoid(x):
    return jax.nn.sigmoid(x)

def _layernorm(x, axis=-1, eps=1e-05):
    m = jnp.mean(x, axis=axis, keepdims=True)
    v = jnp.var(x, axis=axis, keepdims=True)
    return (x - m) / jnp.sqrt(v + eps)

def _scatter_add(tgt, idx, src, axis=0):
    return tgt.at[idx].add(src)

def _segment_sum(src, seg, n):
    return jax.ops.segment_sum(src, seg, n)
kernel_name = 'mk_gnn_preln_d1_gnn_r8_e9d974'

def setup_inputs(seed: int=0):
    np.random.seed(seed)
    _w = jnp.asarray

    def _rec_inputs():
        import jax
        import jax.numpy as jnp
        _gk = jax.random.key(seed)
        x = -0.0002928 + 1 * jax.random.normal(jax.random.fold_in(_gk, 1), (1250, 512), jnp.float32)
        _s = jax.random.randint(jax.random.fold_in(_gk, 2), (20000,), 0, 1250, jnp.int32)
        _d = jax.random.randint(jax.random.fold_in(_gk, 3), (20000,), 0, 1250, jnp.int32)
        _loop = jnp.arange(1250, dtype=jnp.int32)
        src = jnp.concatenate([_s, _d, _loop])
        dst = jnp.concatenate([_d, _s, _loop])
        _o = jnp.argsort(dst, stable=True)
        src = src[_o]
        dst = dst[_o]
        return (x, src, dst)
    x, src, dst = _rec_inputs()

    def _L0_gnn_setup():
        import jax, jax.numpy as jnp
        import numpy as np
        N, IN_DIM, OUT_DIM, H = (1024, 512, 512, 4)
        E = 16384
        HC = H * OUT_DIM
        key = jax.random.key(seed)
        ks = jax.random.split(key, 12)
        s = 1.0 / np.sqrt(IN_DIM)
        return {'x': jax.random.normal(ks[0], (N, IN_DIM), dtype=jnp.float32), 'edge_index': jax.random.randint(ks[1], (2, E), 0, N, dtype=jnp.int64), 'Wq': jax.random.normal(ks[2], (IN_DIM, HC), dtype=jnp.float32) * s, 'bq': jnp.zeros((HC,), dtype=jnp.float32), 'Wk': jax.random.normal(ks[3], (IN_DIM, HC), dtype=jnp.float32) * s, 'bk': jnp.zeros((HC,), dtype=jnp.float32), 'Wv': jax.random.normal(ks[4], (IN_DIM, HC), dtype=jnp.float32) * s, 'bv': jnp.zeros((HC,), dtype=jnp.float32), 'Wskip': jax.random.normal(ks[5], (IN_DIM, HC), dtype=jnp.float32) * s, 'bskip': jnp.zeros((HC,), dtype=jnp.float32), 'Wlin': jax.random.normal(ks[6], (HC, OUT_DIM), dtype=jnp.float32) / np.sqrt(HC), 'blin': jnp.zeros((OUT_DIM,), dtype=jnp.float32), 'gamma': jnp.ones((OUT_DIM,), dtype=jnp.float32), 'beta': jnp.zeros((OUT_DIM,), dtype=jnp.float32)}
    _L0_gnn_all = _L0_gnn_setup()
    _L0_gnn_in = {k: v for k, v in _L0_gnn_all.items() if k in ('Wq', 'bq', 'Wk', 'bk', 'Wv', 'bv', 'Wskip', 'bskip', 'Wlin', 'blin', 'gamma', 'beta')}
    del _L0_gnn_all
    return {'x': x, 'src': src, 'dst': dst, 'L0_gnn_Wq': _L0_gnn_in['Wq'], 'L0_gnn_bq': _L0_gnn_in['bq'], 'L0_gnn_Wk': _L0_gnn_in['Wk'], 'L0_gnn_bk': _L0_gnn_in['bk'], 'L0_gnn_Wv': _L0_gnn_in['Wv'], 'L0_gnn_bv': _L0_gnn_in['bv'], 'L0_gnn_Wskip': _L0_gnn_in['Wskip'], 'L0_gnn_bskip': _L0_gnn_in['bskip'], 'L0_gnn_Wlin': _L0_gnn_in['Wlin'], 'L0_gnn_blin': _L0_gnn_in['blin'], 'L0_gnn_gamma': _L0_gnn_in['gamma'], 'L0_gnn_beta': _L0_gnn_in['beta']}

def reference(x, src, dst, L0_gnn_Wq, L0_gnn_bq, L0_gnn_Wk, L0_gnn_bk, L0_gnn_Wv, L0_gnn_bv, L0_gnn_Wskip, L0_gnn_bskip, L0_gnn_Wlin, L0_gnn_blin, L0_gnn_gamma, L0_gnn_beta):
    import jax
    import jax.numpy as jnp

    def _L0_gnn_ref(x, edge_index, Wq, bq, Wk, bk, Wv, bv, Wskip, bskip, Wlin, blin, gamma, beta):
        import jax, jax.numpy as jnp
        import numpy as np
        N, IN_DIM, OUT_DIM, H = (1024, 512, 512, 4)
        E = 16384
        HC = H * OUT_DIM
        n = x.shape[0]
        src, dst = (edge_index[0], edge_index[1])
        q = (x @ Wq + bq).reshape(n, H, OUT_DIM)
        k = (x @ Wk + bk).reshape(n, H, OUT_DIM)
        v = (x @ Wv + bv).reshape(n, H, OUT_DIM)
        alpha = jnp.einsum('ehc,ehc->eh', q[dst], k[src]) / np.sqrt(OUT_DIM)
        amax = jax.ops.segment_max(alpha, dst, num_segments=n)
        ex = jnp.exp(alpha - amax[dst])
        denom = jax.ops.segment_sum(ex, dst, num_segments=n)
        attn = ex / denom[dst]
        msg = attn[:, :, None] * v[src]
        agg = jax.ops.segment_sum(msg, dst, num_segments=n).reshape(n, HC)
        x_attn = agg + x @ Wskip + bskip
        x_lin = x_attn @ Wlin + blin
        h = x_lin + x_attn[:, :OUT_DIM]
        mu = jnp.mean(h, axis=-1, keepdims=True)
        var = jnp.mean((h - mu) ** 2, axis=-1, keepdims=True)
        return gamma * (h - mu) / jnp.sqrt(var + 1e-05) + beta
    edge_index = jnp.stack([src, dst])
    h = jnp.maximum(_layernorm(x, axis=-1), 0.0)
    x = x + _L0_gnn_ref(h, edge_index, L0_gnn_Wq, L0_gnn_bq, L0_gnn_Wk, L0_gnn_bk, L0_gnn_Wv, L0_gnn_bv, L0_gnn_Wskip, L0_gnn_bskip, L0_gnn_Wlin, L0_gnn_blin, L0_gnn_gamma, L0_gnn_beta)
    return x

_drawn_inputs = setup_inputs


def setup_inputs(seed=0):
    import zlib

    import numpy as np

    out = dict(_drawn_inputs(seed))
    spreads = {'L0_gnn_bq': (0.0, 0.8),
     'L0_gnn_bk': (0.0, 0.8),
     'L0_gnn_bv': (0.0, 0.1),
     'L0_gnn_bskip': (0.0, 0.1),
     'L0_gnn_blin': (0.0, 0.1),
     'L0_gnn_gamma': (1.0, 0.2),
     'L0_gnn_beta': (0.0, 0.1)}
    factors = {}
    for name, (base, spread) in spreads.items():
        noise = np.random.default_rng([zlib.crc32(name.encode()), seed]).standard_normal(out[name].shape)
        drawn = base * np.exp(spread * noise) if base else spread * noise
        out[name] = jnp.asarray(drawn.astype(out[name].dtype))
    for name, factor in factors.items():
        out[name] = (out[name] * factor).astype(out[name].dtype)
    return out
```

```python
from contextlib import ExitStack

import concourse.bass as bass
from concourse import mybir

F32 = mybir.dt.float32
F32R = mybir.dt.float32r
F16 = mybir.dt.float16
I32 = mybir.dt.int32
ALU = mybir.AluOpType
ACT = mybir.ActivationFunctionType
AX_X = mybir.AxisListType.X
RMAX = bass.bass_isa.ReduceOp.max

P = 128
N = 1250
D = 512
H = 4
KT = D // P
NT = (N + P - 1) // P
NP = NT * P
LAST = N - (NT - 1) * P
E = 41250
EP = 125
G = E // (2 * EP)
GB = 3
GR = G // GB
WIN = 32
NW = NP // WIN
SB = (N + 3) // 4
SCALE = float(D) ** -0.5
BIG = 1e30
EPS = 1e-5
CH_N = [(0, 512), (512, 1024), (1024, N)]
CH_NP = [(0, 512), (512, 1024), (1024, NP)]
TG = [(0, 4), (4, 8), (8, NT)]


def rows_of(s):
    return P if s < NT - 1 else LAST


def prepare(nc, io, keep, sem):
    with ExitStack() as ctx:
        sb = lambda name, shape, dt: ctx.enter_context(nc.sbuf_tensor(name, shape, dt))
        xs = sb("xs", [P, NT, D], F32)
        hbuf = sb("hbuf", [P, 2, D], F32)
        stats = sb("stats1", [P, NT, 6], F32)
        mv = sb("mv1", [P, NT, 2], F32)
        std = sb("std1", [P, NT], F32)
        rstd = sb("rstd1", [P, NT], F32)
        nmr = sb("nmr1", [P, NT], F32)
        src_i = sb("src_i", [EP, 2, G], I32)
        dst_i = sb("dst_i", [EP, 2, G], I32)
        dw_i = sb("dw_i", [EP, 2, G], I32)
        srcf = sb("srcf", [EP, 2, G], F32)
        dstf = sb("dstf", [EP, 2, G], F32)
        dwf = sb("dwf", [EP, 2, G], F32)
        blk = sb("blk", [EP, 2, G], F32)
        key0 = sb("key0", [EP, 2, G], F32)
        gmin = sb("gmin", [GR, GB], F32)
        gmax = sb("gmax", [GR, GB], F32)
        win_i = sb("win_i", [P, NW], F32)
        gdown = sb("gdown", [GR, GB], F32)
        gup = sb("gup", [GR, GB], F32)
        flag0 = sb("flag0", [GR, GB, NW], F32)
        flag = sb("flag", [GR, GB, NW], F32)
        vals = sb("vals", [GR, GB, 2, NW], F32)
        val2 = sb("val2", [GR, 2, NW], F32)
        val3 = sb("val3", [GR, 2, NW], F32)
        rng = sb("rng", [GR, 2, NW], F32)
        rlo = sb("rlo", [1, NW], F32)
        rhi = sb("rhi", [1, NW], F32)
        hps = [ctx.enter_context(nc.psum_tensor(f"hps{j}", [P, KT, P], F32)) for j in range(2)]
        gps = [ctx.enter_context(nc.psum_tensor(f"gps{b}", [GR, 2, EP], F32)) for b in range(GB)]

        x_in, edges_in, consts, dve_step = sem("x_in"), sem("edges_in"), sem("consts"), sem("dve_step0")
        std_done, norm_done, h_done, ht_done = sem("std_done"), sem("norm_done"), sem("h_done"), sem("ht_done")
        hi_done, lo_done, gt_done = sem("ht_hi_done"), sem("ht_lo_done"), sem("gt_done")
        vals_done, rng_done, small_in, pad_done = sem("vals_done"), sem("rng_done"), sem("small_in"), sem("pad_done")
        dw_done, stats_done = sem("dw_done"), sem("stats_done")
        block = ctx.enter_context(nc.Block())

        @block.sync
        def _(sp):
            sp.dma_start(src_i[:, :, :], io["src"]).then_inc(edges_in, 16)
            sp.dma_start(dst_i[:, :, :], io["dst"]).then_inc(edges_in, 16)
            sp.dma_start(xs[:, 0:NT - 1, :], io["x"][0:(NT - 1) * P, :].rearrange("(t p) d -> p t d", p=P)).then_inc(x_in, 16)
            sp.wait_ge(pad_done, 1)
            sp.dma_start(xs[0:LAST, NT - 1, :], io["x"][(NT - 1) * P:N, :]).then_inc(x_in, 16)
            for n, name in enumerate(("bq", "bk", "bv", "bs")):
                sp.dma_start(keep["bias"][:, n, :], io[name]).then_inc(small_in, 16)
            sp.wait_ge(small_in, 64)

        @block.gpsimd
        def _(pool):
            nc.gpsimd.memset(xs[:, NT - 1, :], 0.0).then_inc(pad_done, 1)
            nc.gpsimd.memset(keep["ident"][:, :], 1.0).then_inc(pad_done, 1)
            pool.wait_ge(pad_done, 2)
            nc.gpsimd.affine_select(out=keep["ident"][:, :], in_=keep["ident"][:, :], compare_op=ALU.is_equal,
                                    fill=0.0, base=0, pattern=[[-1, P]], channel_multiplier=1).then_inc(consts, 1)
            nc.gpsimd.memset(keep["ones"][:, :], 1.0)
            nc.gpsimd.memset(keep["zero16"][:, :], 0.0)
            nc.gpsimd.iota(keep["iota_col"][:, :], pattern=[[1, SB]], base=0, channel_multiplier=0,
                           allow_small_or_imprecise_dtypes=True).then_inc(consts, 1)
            nc.gpsimd.iota(keep["win_key"][:, :], pattern=[[P, NW]], base=0, channel_multiplier=0,
                           allow_small_or_imprecise_dtypes=True).then_inc(consts, 1)
            nc.gpsimd.iota(win_i[:, :], pattern=[[1, NW]], base=0, channel_multiplier=0,
                           allow_small_or_imprecise_dtypes=True).then_inc(consts, 1)
            nc.gpsimd.iota(gup[:, :], pattern=[[GR, GB]], base=1, channel_multiplier=1,
                           allow_small_or_imprecise_dtypes=True).then_inc(consts, 1)
            nc.gpsimd.iota(gdown[:, :], pattern=[[-GR, GB]], base=G, channel_multiplier=-1,
                           allow_small_or_imprecise_dtypes=True).then_inc(consts, 1)
            pool.wait_ge(vals_done, 1)
            nc.gpsimd.partition_all_reduce(rng[:, :, :].rearrange("p a w -> p (a w)"),
                                           val3[:, :, :].rearrange("p a w -> p (a w)"), GR, RMAX).then_inc(rng_done, 1)

        @block.scalar
        def _(act):
            act.wait_ge(norm_done, 1)
            nc.scalar.activation(std[:, :], std[:, :], ACT.Sqrt).then_inc(std_done, 1)
            act.wait_ge(norm_done, 2)
            for t in range(NT):
                j = t % 2
                if t >= 2:
                    act.wait_ge(ht_done, t - 1)
                nc.scalar.activation(hbuf[:, j, :], xs[:, t, :], ACT.Relu, bias=nmr[:, t:t + 1],
                                     scale=rstd[:, t:t + 1]).then_inc(h_done, 1)
                if t >= 1:
                    act.wait_ge(ht_done, t)
                    nc.scalar.copy(keep["hT_hi"][:, :, (t - 1) * P:t * P], hps[(t - 1) % 2][:, :, :]).then_inc(hi_done, 1)
            act.wait_ge(ht_done, NT)
            nc.scalar.copy(keep["hT_hi"][:, :, (NT - 1) * P:NP], hps[(NT - 1) % 2][:, :, :]).then_inc(hi_done, 1)

        @block.tensor
        def _(pe):
            pe.wait_ge(consts, 1)
            pe.wait_ge(dw_done, 1)
            for b in range(GB):
                for j in range(2):
                    last = nc.tensor.transpose(gps[b][:, j, :], dwf[:, j, b * GR:(b + 1) * GR],
                                               keep["ident"][0:EP, 0:EP])
            last.then_inc(gt_done, 1)
            with pe.Fori(0, NT // 2) as i:
                for j in range(2):
                    t = 2 * i + j
                    pe.wait_ge(h_done, t + 1)
                    pe.wait_ge(lo_done, t + 1)
                    for c in range(KT):
                        last = nc.tensor.transpose(hps[j][:, c, :], hbuf[:, j, c * P:(c + 1) * P], keep["ident"][:, :])
                    last.then_inc(ht_done, 1)

        @block.vector
        def _(dve):
            count = [0]

            def step(ins):
                count[0] += 1
                ins.then_inc(dve_step, 1)
                dve.wait_ge(dve_step, count[0])

            dve.sem_inc(lo_done, 2)
            dve.wait_ge(edges_in, 32)
            nc.vector.tensor_copy(srcf[:, :, :], src_i[:, :, :])
            nc.vector.tensor_copy(dstf[:, :, :], dst_i[:, :, :])
            step(nc.vector.tensor_scalar(dw_i[:, :, :], dst_i[:, :, :], 5, None, ALU.arith_shift_right))
            nc.vector.tensor_copy(dwf[:, :, :], dw_i[:, :, :]).then_inc(dw_done, 1)
            dve.wait_ge(dw_done, 1)
            step(nc.vector.tensor_scalar(blk[:, :, :], srcf[:, :, :], float(SB), None, ALU.is_ge))
            for a in (2, 3):
                step(nc.vector.scalar_tensor_tensor(out=blk[:, :, :], in0=srcf[:, :, :], scalar=float(a * SB),
                                                    in1=blk[:, :, :], op0=ALU.is_ge, op1=ALU.add))
            nc.vector.scalar_tensor_tensor(out=keep["col"][:, :, :], in0=blk[:, :, :], scalar=-float(SB),
                                           in1=srcf[:, :, :], op0=ALU.mult, op1=ALU.add)
            step(nc.vector.scalar_tensor_tensor(out=key0[:, :, :], in0=dwf[:, :, :], scalar=float(P - WIN),
                                                in1=dstf[:, :, :], op0=ALU.mult, op1=ALU.add))
            nc.vector.scalar_tensor_tensor(out=keep["key"][:, :, :], in0=blk[:, :, :], scalar=float(WIN),
                                           in1=key0[:, :, :], op0=ALU.mult, op1=ALU.add)
            dve.wait_ge(gt_done, 1)
            for b in range(GB):
                nc.vector.tensor_reduce(gmin[:, b:b + 1], gps[b][:, :, :].rearrange("p j e -> p (j e)"), AX_X, ALU.min)
                last = nc.vector.tensor_reduce(gmax[:, b:b + 1], gps[b][:, :, :].rearrange("p j e -> p (j e)"), AX_X,
                                               ALU.max)
            step(last)
            dve.wait_ge(consts, 6)
            for b in range(GB):
                step(nc.vector.tensor_scalar(flag0[:, b, :], win_i[0:GR, :], gmin[:, b:b + 1], None, ALU.is_ge))
                step(nc.vector.scalar_tensor_tensor(out=flag[:, b, :], in0=win_i[0:GR, :], scalar=gmax[:, b:b + 1],
                                                    in1=flag0[:, b, :], op0=ALU.is_le, op1=ALU.mult))
                nc.vector.tensor_scalar(vals[:, b, 0, :], flag[:, b, :], gdown[:, b:b + 1], None, ALU.mult)
                step(nc.vector.tensor_scalar(vals[:, b, 1, :], flag[:, b, :], gup[:, b:b + 1], None, ALU.mult))
            step(nc.vector.tensor_tensor(val2[:, :, :], vals[:, 0, :, :], vals[:, 1, :, :], ALU.max))
            nc.vector.tensor_tensor(val3[:, :, :], val2[:, :, :], vals[:, 2, :, :], ALU.max).then_inc(vals_done, 1)

            dve.wait_ge(x_in, 32)
            with dve.Fori(0, NT) as t:
                nc.vector.bn_stats(stats[:, bass.ds(t, 1), :].rearrange("p a b -> p (a b)"),
                                   xs[:, bass.ds(t, 1), :].rearrange("p a b -> p (a b)")).then_inc(stats_done, 1)
            dve.wait_ge(stats_done, NT)
            for t in range(NT):
                last = nc.vector.bn_aggr(mv[:, t, :], stats[:, t, :])
            step(last)
            nc.vector.tensor_scalar(std[:, :], mv[:, :, 1], EPS, None, ALU.add).then_inc(norm_done, 1)
            dve.wait_ge(std_done, 1)
            step(nc.vector.reciprocal(rstd[:, :], std[:, :]))
            nc.vector.scalar_tensor_tensor(out=nmr[:, :], in0=mv[:, :, 0], scalar=-1.0, in1=rstd[:, :],
                                           op0=ALU.mult, op1=ALU.mult).then_inc(norm_done, 1)

            dve.wait_ge(rng_done, 1)
            step(nc.vector.tensor_scalar(rlo[:, :], rng[0:1, 0, :], -1.0, float(G), ALU.mult, ALU.add))
            step(nc.vector.tensor_scalar(rlo[:, :], rlo[:, :], float(G - 1), None, ALU.min))
            step(nc.vector.scalar_tensor_tensor(out=rhi[:, :], in0=rlo[:, :], scalar=1.0, in1=rng[0:1, 1, :],
                                                op0=ALU.add, op1=ALU.max))
            nc.vector.tensor_copy(keep["range"][:, 0, :], rlo[:, :])
            nc.vector.tensor_copy(keep["range"][:, 1, :], rhi[:, :])

            with dve.Fori(0, NT // 2) as i:
                for j in range(2):
                    t = 2 * i + j
                    dve.wait_ge(hi_done, t + 1)
                    nc.vector.tensor_tensor(keep["hT_lo"][:, :, bass.ds(t * P, P)], hps[j][:, :, :],
                                            keep["hT_hi"][:, :, bass.ds(t * P, P)].bitcast(F32),
                                            ALU.subtract).then_inc(lo_done, 1)


def three(nc, out, l_hi, l_lo, r_hi, r_lo, start, stop):
    nc.tensor.matmul(out, l_hi, r_hi, start=start, stop=False, skip_group_check=True)
    nc.tensor.matmul(out, l_hi, r_lo, start=False, stop=False, skip_group_check=True)
    return nc.tensor.matmul(out, l_lo, r_hi, start=False, stop=stop, skip_group_check=True)


QM, KM, VM, SM, LM = range(5)


def fold_weights(nc, io, keep, dram, sem):
    with ExitStack() as ctx:
        sb = lambda name, shape, dt: ctx.enter_context(nc.sbuf_tensor(name, shape, dt))
        raw = [sb(f"raw{j}", [P, KT, D], F32) for j in range(2)]
        w_hi = [sb(f"w_hi{m}", [P, KT, D], F32R) for m in range(5)]
        w_lo = [sb(f"w_lo{m}", [P, KT, D], F32R) for m in range(5)]
        o_hi = sb("o_hi", [P, KT, D], F32R)
        o_lo = sb("o_lo", [P, KT, D], F32R)
        zero = sb("zero_r", [P, D], F32R)
        bias_r = sb("bias_r", [P, 4, H * KT, 2], F32R)
        bkq = sb("bkq", [P, H * KT], F32)
        bkq4 = sb("bkq4", [P, H], F32)
        first = sb("first", [P, H], F32)
        small = sb("small", [P, 8, 8], F32)
        spread = sb("spread", [P, 2 * KT, P], F32)
        prod = [ctx.enter_context(nc.psum_tensor(f"prod{j}", [P, D], F32)) for j in range(2)]
        bps = [ctx.enter_context(nc.psum_tensor(f"bps{m}", [P, D], F32)) for m in range(KT)]
        cols = ctx.enter_context(nc.psum_tensor("cols", [P, 8, 8], F32))
        dots = ctx.enter_context(nc.psum_tensor("dots", [P, H], F32))

        raw_in = [sem(f"raw_in{j}") for j in range(2)]
        raw_free = [sem(f"raw_free{j}") for j in range(2)]
        w_hi_done, w_lo_done = sem("w_hi_done"), sem("w_lo_done")
        qk_used, vsl_used = sem("qk_used"), sem("vsl_used")
        prod_done, prod_hi, prod_lo = sem("prod_done"), sem("prod_hi"), sem("prod_lo")
        stored = [sem(f"stored{m}") for m in range(KT)]
        cols_done, cols_used, bias_ready = sem("cols_done"), sem("cols_used"), sem("bias_ready")
        eye_added, b_done, zero_done, step_d, dots_done = (sem("eye_added"), sem("b_done"), sem("zero_done"),
                                                           sem("dve_step1"), sem("dots_done"))
        small_step = sem("small_step")
        spread_done, rows_done, row_in = sem("spread_done"), sem("rows_done"), sem("row_in")
        block = ctx.enter_context(nc.Block())
        names = ("Wq", "Wk", "Wv", "Ws", "Wl")

        @block.sync
        def _(sp):
            sp.dma_start(keep["s_row"][:, :], io["blin"].partition_broadcast(P)).then_inc(row_in, 16)
            with sp.Fori(0, H) as h:
                for m in range(5):
                    j = m % 2
                    sp.wait_ge(raw_free[j], (3, 2)[j] * h + m // 2 + 1)
                    sp.dma_start(raw[j][:, :, :], io[names[m]][bass.ds(h, 1)].rearrange("a p c n -> (a p) c n")
                                 ).then_inc(raw_in[j], 16)

        @block.gpsimd
        def _(pool):
            nc.gpsimd.memset(zero[:, :].bitcast(F32), 0.0).then_inc(zero_done, 1)
            for j in range(2):
                pool.sem_inc(raw_free[j], 1)
            with pool.Fori(0, H) as h:
                for m in range(5):
                    j = m % 2
                    pool.wait_ge(w_hi_done, 5 * h + m + 1)
                    nc.gpsimd.tensor_tensor(w_lo[m][:, :, :], raw[j][:, :, :], w_hi[m][:, :, :].bitcast(F32),
                                            ALU.subtract).then_inc(w_lo_done, 1)
                    pool.wait_ge(w_lo_done, 5 * h + m + 1)
                    pool.sem_inc(raw_free[j], 1)

        @block.scalar
        def _(act):
            def split_hi(h, m):
                j = m % 2
                act.wait_ge(raw_in[j], 16 * ((3, 2)[j] * h + m // 2 + 1))
                act.wait_ge(qk_used if m in (QM, KM) else vsl_used, h + 1)
                if m == LM:
                    act.wait_ge(eye_added, h + 1)
                nc.scalar.copy(w_hi[m][:, :, :], raw[j][:, :, :]).then_inc(w_hi_done, 1)

            def take_hi(n, m):
                act.wait_ge(prod_done, n + 1)
                act.wait_ge(stored[m], 8 * (n - m) + 32)
                nc.scalar.copy(o_hi[:, m, :], prod[m % 2][:, :]).then_inc(prod_hi, 1)

            def store(n, m, target):
                act.wait_ge(prod_hi, n + 1)
                act.wait_ge(prod_lo, n + 3)
                act.dma_start(target[0][:, m, :], o_hi[:, m, :].bitcast(F32)).then_inc(stored[m], 16)
                act.dma_start(target[1][:, m, :], o_lo[:, m, :].bitcast(F32)).then_inc(stored[m], 16)

            for m in range(KT):
                act.sem_inc(stored[m], 32)
            with act.Fori(0, H) as h:
                for m in range(5):
                    split_hi(h, m)
                for job, to in enumerate(("M", "A")):
                    target = [dram[to][bass.ds(h, 1), half].rearrange("a p c n -> (a p) c n") for half in range(2)]
                    for m in range(KT):
                        take_hi(8 * h + 4 * job + m, m)
                        store(8 * h + 4 * job + m, m, target)
            act.wait_ge(b_done, 1)
            for m in range(KT):
                act.wait_ge(stored[m], 16 * 4 * H + 32)
                nc.scalar.copy(o_hi[:, m, :], bps[m][:, :]).then_inc(prod_hi, 1)
                store(8 * H + m, m, [dram["B"][half] for half in range(2)])
            for m in range(KT):
                act.wait_ge(stored[m], 16 * 4 * H + 64)

        @block.vector
        def _(dve):
            count = [0]

            def step(ins):
                count[0] += 1
                ins.then_inc(step_d, 1)
                dve.wait_ge(step_d, count[0])

            dve.sem_inc(prod_lo, 2)
            bias = keep["bias"]
            step(nc.vector.tensor_copy(bias_r[:, :, :, 0], bias[:, :, :]))
            nc.vector.tensor_tensor(bias_r[:, :, :, 1], bias[:, :, :], bias_r[:, :, :, 0].bitcast(F32), ALU.subtract)
            step(nc.vector.tensor_tensor(bkq[:, :], bias[:, 0, :], bias[:, 1, :], ALU.mult))
            nc.vector.tensor_reduce(bkq4[:, :], bkq[:, :].rearrange("p (h c) -> p h c", h=H), AX_X,
                                    ALU.add).then_inc(bias_ready, 1)
            nc.vector.memset(keep["vs_cols"][:, :], 0.0)
            step(nc.vector.memset(first[:, :], 0.0))
            step(nc.vector.memset(first[:, 0:1], 1.0))
            dve.wait_ge(dots_done, 1)
            nc.vector.tensor_copy(keep["bqbk"][:, :], dots[:, :])

            with dve.Fori(0, H) as h:
                dve.wait_ge(raw_in[0], 16 * (3 * h + 3))
                for c in range(KT):
                    d = raw[0][:, c, c * P:(c + 1) * P]
                    last = nc.vector.scalar_tensor_tensor(out=d, in0=keep["ident"][:, :], scalar=first[:, bass.ds(h, 1)],
                                                          in1=d, op0=ALU.mult, op1=ALU.add)
                last.then_inc(eye_added, 1)
                for n0 in range(2 * KT):
                    m, n = n0 % KT, 8 * h + n0
                    dve.wait_ge(prod_hi, n + 1)
                    nc.vector.tensor_tensor(o_lo[:, m, :], prod[m % 2][:, :], o_hi[:, m, :].bitcast(F32),
                                            ALU.subtract).then_inc(prod_lo, 1)
                dve.wait_ge(cols_done, h + 1)
                nc.vector.tensor_copy(small[:, :, 0:4], cols[:, :, 0:4]).then_inc(small_step, 1)
                dve.wait_ge(small_step, 3 * h + 1)
                nc.vector.tensor_tensor(keep["uw"][:, :, bass.ds(h, 1)].rearrange("p c a -> p (c a)"),
                                        small[:, :, 0], small[:, :, 1], ALU.add)
                nc.vector.tensor_tensor(small[:, :, 2], small[:, :, 2], small[:, :, 3], ALU.add).then_inc(small_step, 1)
                dve.wait_ge(small_step, 3 * h + 2)
                nc.vector.tensor_tensor(keep["vs_cols"][:, :], keep["vs_cols"][:, :], small[:, :, 2],
                                        ALU.add).then_inc(small_step, 1)
                dve.wait_ge(small_step, 3 * h + 3)
                dve.sem_inc(cols_used, 1)
            for i in range(2 * KT):
                last = nc.vector.tensor_scalar(spread[:, i, :], keep["ones"][:, :], keep["vs_cols"][:, i:i + 1], None,
                                               ALU.mult)
            last.then_inc(spread_done, 1)
            dve.wait_ge(rows_done, 1)
            dve.wait_ge(row_in, 16)
            nc.vector.tensor_copy(keep["v_row"][:, :], prod[0][:, :])
            nc.vector.tensor_tensor(keep["s_row"][:, :], prod[1][:, :], keep["s_row"][:, :], ALU.add)
            dve.wait_ge(b_done, 1)
            for m in range(KT):
                dve.wait_ge(prod_hi, 8 * H + m + 1)
                nc.vector.tensor_tensor(o_lo[:, m, :], bps[m][:, :], o_hi[:, m, :].bitcast(F32),
                                        ALU.subtract).then_inc(prod_lo, 1)

        @block.tensor
        def _(pe):
            def product(out, a, b, m, start, stop):
                for c in range(KT):
                    last = three(nc, out, w_hi[a][:, c, m * P:(m + 1) * P], w_lo[a][:, c, m * P:(m + 1) * P],
                                 w_hi[b][:, c, :], w_lo[b][:, c, :], start and c == 0, stop and c == KT - 1)
                return last

            def column(at, a, m, kinds, h):
                for c in range(KT):
                    for half, w in enumerate((w_hi, w_lo)):
                        rhs = bias_r[:, kinds, bass.ds(h * KT + c, 1), :].rearrange("p a b -> p (a b)")
                        last = nc.tensor.matmul(cols[:, at[0], at[1]:at[1] + 2], w[a][:, c, m * P:(m + 1) * P], rhs,
                                                start=(c == 0 and half == 0), stop=(c == KT - 1 and half == 1),
                                                skip_group_check=True)
                return last

            pe.sem_inc(qk_used, 1)
            pe.sem_inc(vsl_used, 1)
            pe.wait_ge(bias_ready, 1)
            nc.tensor.matmul(dots[:, :], keep["ones"][:, :], bkq4[:, :], start=True, stop=True).then_inc(dots_done, 1)
            pe.wait_ge(zero_done, 1)
            for m in range(KT):
                nc.tensor.matmul(bps[m][:, :], zero[:, 0:P], zero[:, :], start=True, stop=False, skip_group_check=True)
            pe.sem_inc(cols_used, 1)
            with pe.Fori(0, H) as h:
                pe.wait_ge(w_lo_done, 5 * h + 2)
                for m in range(KT):
                    pe.wait_ge(prod_lo, 8 * h + m + 1)
                    product(prod[m % 2][:, :], QM, KM, m, True, True).then_inc(prod_done, 1)
                pe.wait_ge(cols_used, h + 1)
                for m in range(KT):
                    column((m, 0), KM, m, 0, h)
                    last = column((KT + m, 0), QM, m, 1, h)
                last.then_inc(qk_used, 1)
                pe.wait_ge(w_lo_done, 5 * h + 5)
                for m in range(KT):
                    pe.wait_ge(prod_lo, 8 * h + KT + m + 1)
                    product(prod[m % 2][:, :], VM, LM, m, True, True).then_inc(prod_done, 1)
                for m in range(KT):
                    product(bps[m][:, :], SM, LM, m, False, False)
                for m in range(KT):
                    column((m, 2), LM, m, 2, h)
                    last = column((KT + m, 2), LM, m, 3, h)
                last.then_inc(cols_done, 1)
                pe.wait_ge(cols_done, h + 1)
                pe.sem_inc(vsl_used, 1)
            for m in range(KT):
                last = nc.tensor.matmul(bps[m][:, :], zero[:, 0:P], zero[:, :], start=False, stop=True,
                                        skip_group_check=True)
            last.then_inc(b_done, 1)
            pe.wait_ge(spread_done, 1)
            pe.wait_ge(prod_lo, 8 * H + 2)
            for n in range(2):
                for m in range(KT):
                    last = nc.tensor.matmul(prod[n][:, m * P:(m + 1) * P], spread[:, n * KT + m, :],
                                            keep["ident"][:, :], start=True, stop=True)
            last.then_inc(rows_done, 1)


def count_edges(nc, keep, dram, sem):
    with ExitStack() as ctx:
        sb = lambda name, shape, dt: ctx.enter_context(nc.sbuf_tensor(name, shape, dt))
        hot_key = [sb(f"hot_key{j}", [EP, P], F16) for j in range(2)]
        hot_col = [sb(f"hot_col{j}", [EP, SB], F16) for j in range(2)]
        logs = [sb(f"logs{s}", [P, 4 * SB], F32) for s in range(2)]
        none = sb("none", [P, N], F32)
        tiny = sb("tiny", [P, 1], F32)
        win = [ctx.enter_context(nc.psum_tensor(f"win{k}", [P, SB], F32)) for k in range(2)]
        hot_ready = [sem(f"hot_ready{j}") for j in range(2)]
        hot_free = [sem(f"hot_free{j}") for j in range(2)]
        win_done, win_free, logs_done, logs_step = sem("win_done"), sem("win_free"), sem("logs_done"), sem("logs_step")
        logs_stored = [sem(f"logs_stored{s}") for s in range(2)]
        tiny_done, logs_ready, pool_turn = sem("tiny_done"), sem("logs_ready"), sem("pool_turn")
        block = ctx.enter_context(nc.Block())

        def window_range(eng, w):
            first = eng.value_load(keep["range"][0:1, 0, bass.ds(w, 1)], min_val=0, max_val=G - 1)
            end = eng.value_load(keep["range"][0:1, 1, bass.ds(w, 1)], min_val=1, max_val=G)
            return first, end

        @block.vector
        def _(dve):
            turn = dve.alloc_register("dve_turn")
            dve.reg_mov(turn, 1)
            with dve.Fori(0, NW) as w:
                first, end = window_range(dve, w)
                with dve.Fori(first, end) as g:
                    n = dve.snap(turn)
                    for j in range(2):
                        dve.wait_ge(hot_free[j], n)
                        nc.vector.tensor_scalar(hot_key[j][:, :], keep["iota_col"][0:EP, 0:P],
                                                keep["win_key"][0:EP, bass.ds(w, 1)],
                                                keep["key"][:, j, bass.ds(g, 1)], ALU.add, ALU.is_equal)
                        nc.vector.tensor_scalar(hot_col[j][:, :], keep["iota_col"][0:EP, :],
                                                keep["col"][:, j, bass.ds(g, 1)], None,
                                                ALU.is_equal).then_inc(hot_ready[j], 1)
                    dve.reg_add(turn, turn, 1)

        @block.tensor
        def _(pe):
            for j in range(2):
                pe.sem_inc(hot_free[j], 1)
            turn = pe.alloc_register("pe_turn")
            pe.reg_mov(turn, 1)
            with pe.Fori(0, NW // 2) as i:
                for k in range(2):
                    w = 2 * i + k
                    first, end = window_range(pe, w)
                    pe.wait_ge(win_free, w + 1)
                    nc.tensor.matmul(win[k][:, :], keep["zero16"][0:EP, 0:P], keep["zero16"][0:EP, 0:SB], start=True,
                                     stop=False, skip_group_check=True)
                    with pe.Fori(first, end):
                        n = pe.snap(turn)
                        for j in range(2):
                            pe.wait_ge(hot_ready[j], n)
                            nc.tensor.matmul(win[k][:, :], hot_key[j][:, :], hot_col[j][:, :], start=False, stop=False,
                                             skip_group_check=True).then_inc(hot_free[j], 1)
                        pe.reg_add(turn, turn, 1)
                    nc.tensor.matmul(win[k][:, :], keep["zero16"][0:EP, 0:P], keep["zero16"][0:EP, 0:SB], start=False,
                                     stop=True, skip_group_check=True).then_inc(win_done, 1)

        @block.scalar
        def _(act):
            act.sem_inc(win_free, 2)
            act.wait_ge(tiny_done, 1)
            with act.Fori(0, NT // 2) as i:
                for s in range(2):
                    t = 2 * i + s
                    act.wait_ge(logs_stored[s], 16 * i + 16)
                    for k in range(4):
                        w = 4 * t + k
                        act.wait_ge(win_done, w + 1)
                        for a in range(4):
                            last = nc.scalar.activation(logs[s][k * WIN:(k + 1) * WIN, a * SB:(a + 1) * SB],
                                                        win[k % 2][a * WIN:(a + 1) * WIN, :], ACT.Ln,
                                                        bias=tiny[a * WIN:(a + 1) * WIN, :])
                        last.then_inc(logs_done, 1)
                        act.wait_ge(logs_done, w + 1)
                        act.sem_inc(win_free, 1)

        @block.gpsimd
        def _(pool):
            nc.gpsimd.memset(tiny[:, :], 2.0 ** -60).then_inc(tiny_done, 1)
            with pool.Fori(0, NT // 2) as i:
                for s in range(2):
                    t = 2 * i + s
                    pool.wait_ge(logs_done, 4 * t + 4)
                    pool.sem_inc(pool_turn, 1)
                    nc.gpsimd.tensor_scalar(none[:, :], logs[s][:, 0:N], -1.0, -BIG, ALU.is_lt, ALU.mult)
                    nc.gpsimd.tensor_scalar(logs[s][:, 0:N], logs[s][:, 0:N], 1.0 / SCALE, None, ALU.mult
                                            ).then_inc(logs_step, 1)
                    pool.wait_ge(logs_step, t + 1)
                    nc.gpsimd.tensor_tensor(logs[s][:, 0:N], logs[s][:, 0:N], none[:, :], ALU.add
                                            ).then_inc(logs_ready, 1)
                    pool.wait_ge(logs_ready, t + 1)

        @block.sync
        def _(sp):
            for s in range(2):
                sp.sem_inc(logs_stored[s], 16)
            with sp.Fori(0, NT // 2) as i:
                for s in range(2):
                    t = 2 * i + s
                    sp.wait_ge(logs_ready, t + 1)
                    sp.dma_start(dram["L"][bass.ds(t, 1)].rearrange("a p n -> (a p) n"), logs[s][:, 0:N]
                                 ).then_inc(logs_stored[s], 16)
            for s in range(2):
                sp.wait_ge(logs_stored[s], 16 * (NT // 2) + 16)


def attend(nc, io, keep, dram, sem):
    with ExitStack() as ctx:
        sb = lambda name, shape, dt: ctx.enter_context(nc.sbuf_tensor(name, shape, dt))
        m_r = [sb(f"m_{x}", [P, KT, D], F32R) for x in ("hi", "lo")]
        a_r = [sb(f"a_{x}", [P, KT, D], F32R) for x in ("hi", "lo")]
        g_r = [sb(f"g_{x}", [P, NT, D], F32R) for x in ("hi", "lo")]
        qt_r = [sb(f"qt_{x}", [P, KT, P], F32R) for x in ("hi", "lo")]
        pt_r = [sb(f"pt_{x}", [P, NT, P], F32R) for x in ("hi", "lo")]
        q = sb("q", [P, KT, NP], F32)
        y = sb("y", [P, NT, D], F32)
        probs = sb("probs", [P, N], F32)
        logs = sb("logs_in", [P, N], F32)
        w_r = sb("w_r", [P, KT, 2, H], F32R)
        r = sb("r", [P, H * NT], F32)
        rs = sb("rs", [P, H * NT], F32)
        r2 = sb("r2", [P, NT, 2 * H], F32)
        r3 = sb("r3", [P, NT, H], F32)
        has = sb("has", [P, NT], F32)
        u = sb("u", [P, KT], F32)
        mx, amax, shift, den, total, share = (sb(x, [P, 1], F32) for x in ("mx", "amax", "shift", "den", "total", "share"))
        gamma = sb("gamma", [P, D], F32)
        beta = sb("beta", [P, D], F32)
        stats = sb("stats2", [P, NT, 6], F32)
        mv = sb("mv2", [P, NT, 2], F32)
        std = sb("std2", [P, NT], F32)
        rstd = sb("rstd2", [P, NT], F32)
        nmr = sb("nmr2", [P, NT], F32)
        x = q[:, :, :].rearrange("p c n -> p (c n)").rearrange("p (t d) -> p t d", t=NT)
        h_r = (keep["hT_hi"], keep["hT_lo"])

        sps = ctx.enter_context(nc.psum_tensor("sps", [P, 3 * 512], F32))
        tps = [ctx.enter_context(nc.psum_tensor(f"tps{g}", [P, 4, P], F32)) for g in range(len(TG))]
        wps = [ctx.enter_context(nc.psum_tensor(f"wps{b}", [P, 512], F32)) for b in range(2)]

        m_in, a_in, logs_in, row_in, x_in = sem("m_in"), sem("a_in"), sem("logs_arrived"), sem("row_in2"), sem("x_in2")
        m_used, a_used, logs_used = sem("m_used"), sem("a_used"), sem("logs_used")
        w_done = [sem(f"w_done{b}") for b in range(2)]
        w_free = [sem(f"w_free{b}") for b in range(2)]
        q_done, qt_hi, qt_lo, g_hi, g_lo = sem("q_done"), sem("qt_hi_done"), sem("qt_lo_done"), sem("g_hi_done"), sem("g_lo_done")
        s_done, shift_done, exp_done = sem("s_done"), sem("shift_done"), sem("exp_done")
        t_done, pt_hi, pt_lo, y_done = sem("t_done"), sem("pt_hi_done"), sem("pt_lo_done"), sem("y_done")
        w_r_done, r_done, r_ready = sem("w_r_done"), sem("r_done"), sem("r_ready")
        chain, mx_done, amax_done, total_done, share_done = (sem("chain"), sem("mx_done"), sem("amax_done"),
                                                           sem("total_done"), sem("share_done"))
        u_done, row_turn = sem("u_done"), sem("row_turn")
        st_done, mv_done, yb_done = sem("st_done"), sem("mv_done"), sem("yb_done")
        var_done, std_done, norm_ready = sem("var_done"), sem("std_done2"), sem("norm_ready")
        z_done, zg_done, xb_done, out_ready, out_stored = (sem("z_done"), sem("zg_done"), sem("xb_done"),
                                                           sem("out_ready"), sem("out_stored"))
        block = ctx.enter_context(nc.Block())
        W0, W1, START = 11 + NT, 11, NT // 2

        def use(h, i):
            return START + (W0, W1)[i % 2] * h + i // 2

        def use_pv(h, t):
            return START + W0 * h + 11 + t

        @block.sync
        def _(sp):
            sp.dma_start(gamma[:, :], io["gamma"].partition_broadcast(P)).then_inc(row_in, 16)
            sp.dma_start(beta[:, :], io["beta"].partition_broadcast(P)).then_inc(row_in, 16)
            with sp.Fori(0, H) as h:
                with sp.Fori(0, NT) as t:
                    sp.wait_ge(logs_used, NT * h + t + 1)
                    sp.dma_start(logs[:, :], dram["L"][bass.ds(t, 1)].rearrange("a p n -> (a p) n")
                                 ).then_inc(logs_in, 16)
            sp.wait_ge(s_done, H * NT + 1)
            sp.dma_start(x[:, 0:NT - 1, :], io["x"][0:(NT - 1) * P, :].rearrange("(t p) d -> p t d", p=P)
                         ).then_inc(x_in, 16)
            sp.dma_start(x[0:LAST, NT - 1, :], io["x"][(NT - 1) * P:N, :]).then_inc(x_in, 16)
            with sp.Fori(0, NT - 1) as t:
                sp.wait_ge(out_ready, t + 1)
                sp.dma_start(io["out"][bass.ds(t * P, P), :], y[:, bass.ds(t, 1), :].rearrange("p a d -> p (a d)")
                             ).then_inc(out_stored, 16)
            sp.wait_ge(out_ready, NT)
            sp.dma_start(io["out"][(NT - 1) * P:N, :], y[0:LAST, NT - 1, :]).then_inc(out_stored, 16)
            sp.wait_ge(out_stored, 16 * NT)

        @block.gpsimd
        def _(pool):
            for half in range(2):
                pool.dma_start(a_r[half][:, :, :].bitcast(F32), dram["B"][half]).then_inc(a_in, 16)
            for h in range(H):
                pool.wait_ge(m_used, h + 1)
                for half in range(2):
                    pool.dma_start(m_r[half][:, :, :].bitcast(F32), dram["M"][h, half]).then_inc(m_in, 16)
                pool.wait_ge(a_used, h + 1)
                for half in range(2):
                    pool.dma_start(a_r[half][:, :, :].bitcast(F32), dram["A"][h, half]).then_inc(a_in, 16)
            pool.wait_ge(x_in, 32)
            pool.wait_ge(row_in, 32)
            for t in range(NT):
                p = rows_of(t)
                nc.gpsimd.tensor_tensor(x[0:p, t, :], x[0:p, t, :], beta[0:p, :], ALU.add).then_inc(xb_done, 1)

        @block.tensor
        def _(pe):
            def scores(c, n):
                a, b = CH_N[c]
                for k in range(KT):
                    last = three(nc, sps[:, a:b], qt_r[0][:, k, :], qt_r[1][:, k, :], h_r[0][:, k, a:b],
                                 h_r[1][:, k, a:b], k == 0, k == KT - 1)
                if c == len(CH_N) - 1:
                    last.then_inc(s_done, 1)

            def transposes(g, n):
                pe.wait_ge(pt_lo, 3 * n + g + 1)
                a, b = TG[g]
                for s in range(a, b):
                    last = nc.tensor.transpose(tps[g][0:rows_of(s), s - a, :], probs[:, s * P:s * P + rows_of(s)],
                                               keep["ident"][:, :])
                last.then_inc(t_done, 1)

            def apply(h, t, n):
                pe.wait_ge(w_free[0], use_pv(h, t) + 1)
                pe.wait_ge(g_lo, NT * h + NT)
                for g, (a, b) in enumerate(TG):
                    pe.wait_ge(pt_lo, 3 * n + g + 4)
                    for s in range(a, b):
                        p = rows_of(s)
                        last = three(nc, wps[0][:, :], pt_r[0][0:p, s, :], pt_r[1][0:p, s, :], g_r[0][0:p, s, :],
                                     g_r[1][0:p, s, :], s == 0, s == NT - 1)
                last.then_inc(w_done[0], 1)

            def rows_times(s, i, before):
                b = i % 2
                pe.wait_ge(w_free[b], before + 1)
                for k in range(KT):
                    last = three(nc, wps[b][:, :], h_r[0][:, k, s * P:(s + 1) * P], h_r[1][:, k, s * P:(s + 1) * P],
                                 a_r[0][:, k, :], a_r[1][:, k, :], k == 0, k == KT - 1)
                last.then_inc(w_done[b], 1)

            pe.sem_inc(m_used, 1)
            pe.sem_inc(s_done, 1)
            pe.wait_ge(w_r_done, 1)
            for s in range(NT):
                for k in range(KT):
                    for half in range(2):
                        last = nc.tensor.matmul(sps[:, s * 8:s * 8 + 8], h_r[half][:, k, s * P:(s + 1) * P],
                                                w_r[:, k, :, :].rearrange("p a h -> p (a h)"),
                                                start=(k == 0 and half == 0), stop=(k == KT - 1 and half == 1))
            last.then_inc(r_done, 1)
            pe.wait_ge(a_in, 32)
            for s in range(NT):
                rows_times(s, s, s // 2)
            pe.wait_ge(w_done[1], START)
            pe.sem_inc(a_used, 1)
            pe.wait_ge(r_ready, 1)
            with pe.Fori(0, H) as h:
                pe.wait_ge(m_in, 32 * h + 32)
                for m in range(KT):
                    for c, (a, b) in enumerate(CH_NP):
                        i = 3 * m + c
                        pe.wait_ge(w_free[i % 2], use(h, i) + 1)
                        for k in range(KT):
                            last = three(nc, wps[i % 2][:, 0:b - a], m_r[0][:, k, m * P:(m + 1) * P],
                                         m_r[1][:, k, m * P:(m + 1) * P], h_r[0][:, k, a:b], h_r[1][:, k, a:b],
                                         k == 0, k == KT - 1)
                        last.then_inc(w_done[i % 2], 1)
                pe.wait_ge(w_done[1], use(h, 11) + 1)
                pe.sem_inc(m_used, 1)
                pe.wait_ge(a_in, 32 * h + 64)
                for s in range(NT // 2):
                    rows_times(s, 12 + s, use(h, 12 + s))
                pe.wait_ge(qt_lo, NT * h + 1)
                for c in range(len(CH_N)):
                    scores(c, NT * h)
                for s in range(NT // 2, NT):
                    rows_times(s, 12 + s, use(h, 12 + s))
                pe.wait_ge(w_done[1], use(h, 21) + 1)
                pe.sem_inc(a_used, 1)
                with pe.Fori(0, NT - 1) as t:
                    n = NT * h + t
                    pe.wait_ge(exp_done, n + 1)
                    for g in range(len(TG)):
                        transposes(g, n)
                        if g == 0:
                            pe.wait_ge(qt_lo, n + 2)
                        scores(g, n + 1)
                    apply(h, t, n)
                n = NT * h + NT - 1
                pe.wait_ge(exp_done, n + 1)
                for g in range(len(TG)):
                    transposes(g, n)
                apply(h, NT - 1, n)

        @block.scalar
        def _(act):
            def q_hi(h, t, n):
                act.wait_ge(s_done, n + 1)
                nc.scalar.copy(qt_r[0][:, :, :], q[:, :, bass.ds(t * P, P)]).then_inc(qt_hi, 1)

            def softmax(n):
                act.wait_ge(shift_done, n + 1)
                nc.scalar.activation(probs[:, :], sps[:, 0:N], ACT.Exp, bias=shift[:, :], scale=SCALE,
                                     accum_out=den[:, :]).then_inc(exp_done, 1)

            def take_g(h, s):
                i = 12 + s
                act.wait_ge(w_done[i % 2], use(h, i) + 1)
                nc.scalar.copy(g_r[0][:, s, :], wps[i % 2][:, :]).then_inc(g_hi, 1)

            def take_pt(n):
                for g, (a, b) in enumerate(TG):
                    act.wait_ge(t_done, 3 * n + g + 1)
                    whole = [s for s in range(a, b) if rows_of(s) == P]
                    z = a + len(whole)
                    last = nc.scalar.copy(pt_r[0][:, a:z, :], tps[g][:, 0:z - a, :])
                    if z < b:
                        last = nc.scalar.copy(pt_r[0][0:LAST, z, :], tps[g][0:LAST, z - a, :])
                    last.then_inc(pt_hi, 1)

            act.sem_inc(w_free[0], 1)
            act.sem_inc(w_free[1], 1)
            with act.Fori(0, H) as h:
                nc.scalar.copy(u[:, :], keep["uw"][:, 0:KT, bass.ds(h, 1)].rearrange("p c a -> p (c a)")
                               ).then_inc(u_done, 1)
                act.wait_ge(u_done, h + 1)
                for m in range(KT):
                    for c, (a, b) in enumerate(CH_NP):
                        i = 3 * m + c
                        act.wait_ge(w_done[i % 2], use(h, i) + 1)
                        nc.scalar.activation(q[:, m, a:b], wps[i % 2][:, 0:b - a], ACT.Identity,
                                             bias=u[:, m:m + 1]).then_inc(w_free[i % 2], 1)
                act.wait_ge(w_free[0], use(h, 10) + 2)
                act.wait_ge(w_free[1], use(h, 11) + 2)
                q_hi(h, 0, NT * h)
                for s in range(NT // 2):
                    take_g(h, s)
                q_hi(h, 1, NT * h + 1)
                take_g(h, NT // 2)
                softmax(NT * h)
                for s in range(NT // 2 + 1, NT):
                    take_g(h, s)
                with act.Fori(0, NT - 2) as t:
                    n = NT * h + t
                    take_pt(n)
                    q_hi(h, t + 2, n + 2)
                    softmax(n + 1)
                n = NT * h + NT - 2
                take_pt(n)
                softmax(n + 1)
                take_pt(n + 1)
            act.wait_ge(var_done, 1)
            nc.scalar.activation(std[:, :], std[:, :], ACT.Sqrt).then_inc(std_done, 1)
            act.wait_ge(norm_ready, 1)
            for t in range(NT):
                nc.scalar.activation(y[:, t, :], y[:, t, :], ACT.Identity, bias=nmr[:, t:t + 1],
                                     scale=rstd[:, t:t + 1]).then_inc(z_done, 1)

        @block.vector
        def _(dve):
            def q_lo(t, n):
                dve.wait_ge(qt_hi, n + 1)
                nc.vector.tensor_tensor(qt_r[1][:, :, :], q[:, :, bass.ds(t * P, P)], qt_r[0][:, :, :].bitcast(F32),
                                        ALU.subtract).then_inc(qt_lo, 1)

            def row_max(n):
                dve.wait_ge(share_done, n + 1)
                dve.wait_ge(s_done, n + 2)
                dve.wait_ge(logs_in, 16 * n + 16)
                dve.sem_inc(row_turn, 1)
                nc.vector.tensor_tensor_reduce(sps[:, 0:N], sps[:, 0:N], logs[:, :], 1.0, -BIG / 2, ALU.add, ALU.max,
                                               mx[:, :]).then_inc(mx_done, 1)
                dve.wait_ge(mx_done, n + 1)
                dve.sem_inc(logs_used, 1)
                nc.vector.tensor_scalar(amax[:, :], mx[:, :], r[:, bass.ds(n, 1)], SCALE, ALU.add, ALU.mult
                                        ).then_inc(amax_done, 1)
                dve.wait_ge(amax_done, n + 1)
                nc.vector.tensor_tensor(shift[:, :], rs[:, bass.ds(n, 1)], amax[:, :], ALU.subtract).then_inc(shift_done, 1)

            def split_g(h, s):
                i = 12 + s
                dve.wait_ge(g_hi, NT * h + s + 1)
                nc.vector.tensor_tensor(g_r[1][:, s, :], wps[i % 2][:, :], g_r[0][:, s, :].bitcast(F32),
                                        ALU.subtract).then_inc(w_free[i % 2], 1)
                if s == NT - 1:
                    dve.wait_ge(w_free[1], use(h, 21) + 2)
                    dve.sem_inc(g_lo, NT)

            def split_pt(n):
                for g, (a, b) in enumerate(TG):
                    dve.wait_ge(pt_hi, 3 * n + g + 1)
                    z = a + len([s for s in range(a, b) if rows_of(s) == P])
                    last = nc.vector.tensor_tensor(pt_r[1][:, a:z, :], tps[g][:, 0:z - a, :],
                                                   pt_r[0][:, a:z, :].bitcast(F32), ALU.subtract)
                    if z < b:
                        last = nc.vector.tensor_tensor(pt_r[1][0:LAST, z, :], tps[g][0:LAST, z - a, :],
                                                       pt_r[0][0:LAST, z, :].bitcast(F32), ALU.subtract)
                    last.then_inc(pt_lo, 1)

            def take_share(t, n):
                dve.wait_ge(exp_done, n + 1)
                nc.vector.tensor_scalar(has[:, bass.ds(t, 1)], den[:, :], 0.0, None, ALU.is_gt)
                nc.vector.tensor_scalar(total[:, :], den[:, :], 2.0 ** -60, None, ALU.max).then_inc(total_done, 1)
                dve.wait_ge(total_done, n + 1)
                nc.vector.reciprocal(share[:, :], total[:, :]).then_inc(share_done, 1)

            def add_head(h, t, n):
                dve.wait_ge(share_done, n + 2)
                dve.wait_ge(w_done[0], use_pv(h, t) + 1)
                yt = y[:, bass.ds(t, 1), :].rearrange("p a d -> p (a d)")
                nc.vector.scalar_tensor_tensor(out=yt, in0=wps[0][:, :], scalar=share[:, :], in1=yt, op0=ALU.mult,
                                               op1=ALU.add).then_inc(w_free[0], 1)

            count = [0]

            def step(ins):
                count[0] += 1
                ins.then_inc(chain, 1)
                dve.wait_ge(chain, count[0])

            dve.sem_inc(pt_lo, 3)
            dve.sem_inc(logs_used, 1)
            dve.sem_inc(share_done, 1)
            w = keep["uw"][:, KT:2 * KT, :]
            step(nc.vector.tensor_copy(w_r[:, :, 0, :], w))
            nc.vector.tensor_tensor(w_r[:, :, 1, :], w, w_r[:, :, 0, :].bitcast(F32), ALU.subtract).then_inc(w_r_done, 1)
            dve.wait_ge(r_done, 1)
            step(nc.vector.tensor_copy(r2[:, :, :], sps[:, 0:8 * NT].rearrange("p (t a) -> p t a", t=NT)))
            step(nc.vector.tensor_tensor(r3[:, :, :], r2[:, :, 0:H], r2[:, :, H:2 * H], ALU.add))
            for h in range(H):
                last = nc.vector.tensor_scalar(r[:, h * NT:(h + 1) * NT], r3[:, :, h], keep["bqbk"][:, h:h + 1], None,
                                               ALU.add)
            step(last)
            nc.vector.tensor_scalar(rs[:, :], r[:, :], SCALE, None, ALU.mult).then_inc(r_ready, 1)
            dve.wait_ge(r_ready, 1)
            for s in range(NT):
                dve.wait_ge(w_done[s % 2], s // 2 + 1)
                last = nc.vector.tensor_tensor(y[:, s, :], wps[s % 2][:, :], keep["s_row"][:, :], ALU.add)
                last.then_inc(w_free[s % 2], 1)
            with dve.Fori(0, H) as h:
                q_lo(0, NT * h)
                for s in range(NT // 2):
                    split_g(h, s)
                row_max(NT * h)
                q_lo(1, NT * h + 1)
                for s in range(NT // 2, NT):
                    split_g(h, s)
                with dve.Fori(0, NT - 2) as t:
                    n = NT * h + t
                    take_share(t, n)
                    split_pt(n)
                    row_max(n + 1)
                    q_lo(t + 2, n + 2)
                    add_head(h, t, n)
                n = NT * h + NT - 2
                take_share(NT - 2, n)
                split_pt(n)
                row_max(n + 1)
                add_head(h, NT - 2, n)
                take_share(NT - 1, n + 1)
                split_pt(n + 1)
                add_head(h, NT - 1, n + 1)
            dve.wait_ge(w_free[0], START + W0 * H + 1)
            with dve.Fori(0, NT) as t:
                yt = y[:, bass.ds(t, 1), :].rearrange("p a d -> p (a d)")
                nc.vector.scalar_tensor_tensor(out=yt, in0=keep["v_row"][:, :], scalar=has[:, bass.ds(t, 1)], in1=yt,
                                               op0=ALU.mult, op1=ALU.add).then_inc(yb_done, 1)
                dve.wait_ge(yb_done, t + 1)
                nc.vector.bn_stats(stats[:, bass.ds(t, 1), :].rearrange("p a b -> p (a b)"), yt).then_inc(st_done, 1)
            dve.wait_ge(st_done, NT)
            for t in range(NT):
                last = nc.vector.bn_aggr(mv[:, t, :], stats[:, t, :])
            last.then_inc(mv_done, 1)
            dve.wait_ge(mv_done, 1)
            nc.vector.tensor_scalar(std[:, :], mv[:, :, 1], EPS, None, ALU.add).then_inc(var_done, 1)
            dve.wait_ge(std_done, 1)
            step(nc.vector.reciprocal(rstd[:, :], std[:, :]))
            nc.vector.scalar_tensor_tensor(out=nmr[:, :], in0=mv[:, :, 0], scalar=-1.0, in1=rstd[:, :], op0=ALU.mult,
                                           op1=ALU.mult).then_inc(norm_ready, 1)
            dve.wait_ge(row_in, 32)
            for t in range(NT):
                p = rows_of(t)
                dve.wait_ge(z_done, t + 1)
                nc.vector.tensor_tensor(y[0:p, t, :], y[0:p, t, :], gamma[0:p, :], ALU.mult).then_inc(zg_done, 1)
                dve.wait_ge(zg_done, t + 1)
                dve.wait_ge(xb_done, t + 1)
                nc.vector.tensor_tensor(y[0:p, t, :], y[0:p, t, :], x[0:p, t, :], ALU.add).then_inc(out_ready, 1)


def build(nc, io):
    with ExitStack() as ctx:
        keep_sb = lambda name, shape, dt: ctx.enter_context(nc.sbuf_tensor(name, shape, dt))
        sem = lambda name: ctx.enter_context(nc.semaphore(name))
        keep = {
            "hT_hi": keep_sb("hT_hi", [P, KT, NP], F32R),
            "hT_lo": keep_sb("hT_lo", [P, KT, NP], F32R),
            "ident": keep_sb("ident", [P, P], F32),
            "uw": keep_sb("uw", [P, 2 * KT, H], F32),
            "vs_cols": keep_sb("vs_cols", [P, 2 * KT], F32),
            "bqbk": keep_sb("bqbk", [P, H], F32),
            "v_row": keep_sb("v_row", [P, D], F32),
            "s_row": keep_sb("s_row", [P, D], F32),
        }
        r32 = lambda name, shape: nc.dram_tensor(name, shape, F32).ap()
        dram = {
            "M": r32("M_parts", [H, 2, P, KT, D]),
            "A": r32("A_parts", [H, 2, P, KT, D]),
            "B": r32("B_parts", [2, P, KT, D]),
            "L": nc.dram_tensor("log_counts", [NT, P, N], F32).ap(),
        }
        with ExitStack() as early:
            early_sb = lambda name, shape, dt: early.enter_context(nc.sbuf_tensor(name, shape, dt))
            keep |= {
                "ones": early_sb("ones", [P, P], F32),
                "zero16": early_sb("zero16", [P, SB], F16),
                "iota_col": early_sb("iota_col", [P, SB], F16),
                "win_key": early_sb("win_key", [P, NW], F32),
                "key": early_sb("key", [EP, 2, G], F32),
                "col": early_sb("col", [EP, 2, G], F32),
                "range": early_sb("range", [1, 2, NW], I32),
                "bias": early_sb("bias", [P, 4, H * KT], F32),
            }
            with ExitStack() as sems:
                prepare(nc, io, keep, lambda name: sems.enter_context(nc.semaphore(name)))
            with ExitStack() as sems:
                fold_weights(nc, io, keep, dram, lambda name: sems.enter_context(nc.semaphore(name)))
            with ExitStack() as sems:
                count_edges(nc, keep, dram, lambda name: sems.enter_context(nc.semaphore(name)))
        attend(nc, io, keep, dram, sem)


def kernel(x, src, dst, L0_gnn_Wq, L0_gnn_bq, L0_gnn_Wk, L0_gnn_bk, L0_gnn_Wv, L0_gnn_bv, L0_gnn_Wskip, L0_gnn_bskip,
           L0_gnn_Wlin, L0_gnn_blin, L0_gnn_gamma, L0_gnn_beta):
    import numpy as np
    import concourse.bacc as bacc
    from concourse.bass_utils import run_bass_kernel_spmd

    tiled = lambda w: np.ascontiguousarray(np.asarray(w).reshape(H, KT, P, D).transpose(0, 2, 1, 3))
    edges = lambda e: np.ascontiguousarray(np.asarray(e).reshape(G, 2, EP).transpose(2, 1, 0))
    column = lambda b: np.ascontiguousarray(np.asarray(b).reshape(H * KT, P).T)
    arrays = {
        "x": np.ascontiguousarray(x), "src": edges(src), "dst": edges(dst),
        "Wq": tiled(np.asarray(L0_gnn_Wq).T), "Wk": tiled(np.asarray(L0_gnn_Wk).T),
        "Wv": tiled(np.asarray(L0_gnn_Wv).T), "Ws": tiled(np.asarray(L0_gnn_Wskip).T), "Wl": tiled(L0_gnn_Wlin),
        "bq": column(L0_gnn_bq), "bk": column(L0_gnn_bk), "bv": column(L0_gnn_bv), "bs": column(L0_gnn_bskip),
        "blin": np.ascontiguousarray(L0_gnn_blin), "gamma": np.ascontiguousarray(L0_gnn_gamma),
        "beta": np.ascontiguousarray(L0_gnn_beta),
    }
    nc = bacc.Bacc("TRN2", target_bir_lowering=False, num_devices=1)
    io = {name: nc.dram_tensor(f"in_{name}", a.shape, mybir.dt.from_np(a.dtype), kind="ExternalInput").ap()
          for name, a in arrays.items()}
    io["out"] = nc.dram_tensor("out", (N, D), F32, kind="ExternalOutput").ap()
    build(nc, io)
    result = run_bass_kernel_spmd(nc, [{f"in_{name}": a for name, a in arrays.items()}], core_ids=[0])
    return result.results[0]["out"]
```

```python
from contextlib import ExitStack

import concourse.bass as bass
from concourse import mybir

F32 = mybir.dt.float32
F32R = mybir.dt.float32r
F16 = mybir.dt.float16
I32 = mybir.dt.int32
ALU = mybir.AluOpType
ACT = mybir.ActivationFunctionType
AX_X = mybir.AxisListType.X
RMAX = bass.bass_isa.ReduceOp.max

P = 128
N = 1250
D = 512
H = 4
KT = D // P
NT = (N + P - 1) // P
NP = NT * P
LAST = N - (NT - 1) * P
E = 41250
EP = 125
J = 5
G = E // (J * EP)
SLOTS = 2
WIN = 32
NW = NP // WIN
SB = (N + 3) // 4
SCALE = float(D) ** -0.5
BIG = 1e30
EPS = 1e-5
CH_N = [(0, 512), (512, 1024), (1024, N)]
CH_NP = [(0, 512), (512, 1024), (1024, NP)]
TG = [(0, 4), (4, 8), (8, NT)]


def rows_of(s):
    return P if s < NT - 1 else LAST


def three(nc, out, l_hi, l_lo, r_hi, r_lo, start, stop):
    nc.tensor.matmul(out, l_hi, r_hi, start=start, stop=False, skip_group_check=True)
    nc.tensor.matmul(out, l_hi, r_lo, start=False, stop=False, skip_group_check=True)
    return nc.tensor.matmul(out, l_lo, r_hi, start=False, stop=stop, skip_group_check=True)


QM, KM, VM, LM, SM = range(5)
NAMES = ("Wq", "Wk", "Wv", "Wl", "Ws")
PAIR = {QM: 0, KM: 1, VM: 2, LM: 3, SM: 1}
WORK = ([], [("M", 0)], [("M", 1), ("M", 2)], [("uw", 0), ("M", 3)], [("A", 0)], [("A", 1), ("A", 2)], [("A", 3)],
        [("B", 0), ("B", 1)], [("B", 2)], [("vs", 0), ("B", 3)])
SPLIT = {0: (QM, KM), 1: (VM,), 2: (LM,), 4: (SM,)}
WH = NW // H
TILE_WINS = P // WIN
UNROLL = 2
MOST_GROUPS = NW * G


def fold_and_count(nc, io, keep, dram, sem):
    with ExitStack() as ctx:
        sb = lambda name, shape, dt: ctx.enter_context(nc.sbuf_tensor(name, shape, dt))
        raw = [sb(f"raw{j}", [P, KT, D], F32) for j in range(2)]
        w_hi = [sb(f"w_hi{m}", [P, KT, D], F32R) for m in range(4)]
        w_lo = [sb(f"w_lo{m}", [P, KT, D], F32R) for m in range(4)]
        o_hi = sb("o_hi", [P, KT, D], F32R)
        o_lo = sb("o_lo", [P, KT, D], F32R)
        xs = sb("xs", [P, NT, D], F32)
        zero = sb("zero_r", [P, D], F32R)
        ones = sb("ones", [P, P], F32)
        zero16 = sb("zero16", [EP, SB], F16)
        iota_key = sb("iota_key", [EP, J, P], F16)
        iota_col = sb("iota_col", [EP, SB], F16)
        win_key = sb("win_key", [EP, NW], F32)
        hot_key = sb("hot_key", [EP, SLOTS, J, P], F16)
        hot_col = sb("hot_col", [EP, SLOTS, J, SB], F16)
        key = sb("key", [EP, J, G], F32)
        col = sb("col", [EP, J, G], F32)
        src_i = sb("src_i", [EP, J, G], I32)
        dst_i = sb("dst_i", [EP, J, G], I32)
        dw_i = sb("dw_i", [EP, J, G], I32)
        srcf = sb("srcf", [EP, J, G], F32)
        dstf = sb("dstf", [EP, J, G], F32)
        dwf = sb("dwf", [EP, J, G], F32)
        blk = sb("blk", [EP, J, G], F32)
        bias = sb("bias", [P, 4, H * KT], F32)
        bias_r = sb("bias_r", [P, 4, H * KT, 2], F32R)
        bkq = sb("bkq", [P, H * KT], F32)
        bkq4 = sb("bkq4", [P, H], F32)
        first = sb("first", [P, H], F32)
        small = sb("small", [P, 8, 8], F32)
        vs_cols = sb("vs_cols", [P, 2 * KT], F32)
        tiny = sb("tiny", [P, 1], F32)
        stats = sb("stats1", [P, NT, 6], F32)
        mv = sb("mv1", [P, NT, 2], F32)
        std, rstd, nmr = (sb(f"{x}1", [P, NT], F32) for x in ("std", "rstd", "nmr"))
        ends2 = sb("ends2", [G, 2, 2], F32)
        ends = sb("ends", [G, 2], F32)
        win_i = sb("win_i", [G, NW], F32)
        gdown, gup = sb("gdown", [G, 1], F32), sb("gup", [G, 1], F32)
        flag0, flag = sb("flag0", [G, NW], F32), sb("flag", [G, NW], F32)
        vals, rng = sb("vals", [G, 2, NW], F32), sb("rng", [G, 2, NW], F32)
        rlo, rhi = sb("rlo", [1, NW], F32), sb("rhi", [1, NW], F32)
        win_range = sb("win_range", [1, 2, NW], I32)
        flat = xs[:, :, :].rearrange("p t d -> p (t d)")
        logs = [flat[:, s * 4 * SB:(s + 1) * 4 * SB] for s in range(2)]
        none = flat[:, 8 * SB:8 * SB + N]
        spread = flat[:, 0:2 * KT * P].rearrange("p (i n) -> p i n", i=2 * KT)

        prod = [ctx.enter_context(nc.psum_tensor(f"prod{j}", [P, D], F32)) for j in range(2)]
        bps = [ctx.enter_context(nc.psum_tensor(f"bps{m}", [P, D], F32)) for m in range(KT)]
        wbank = [ctx.enter_context(nc.psum_tensor(f"wbank{k}", [P, D], F32)) for k in range(2)]
        win = [b[:, 0:SB] for b in wbank]
        cols = wbank[0][:, 384:384 + 64].rearrange("p (a b) -> p a b", a=8)
        dots = wbank[0][:, 448:448 + H]
        hps = [b[:, :].rearrange("p (c n) -> p c n", c=KT) for b in prod]
        gps = [bps[0][0:G, 0:3 * EP], bps[1][0:G, 0:2 * EP]]

        edges_in, x_in, bias_in, row_in = sem("edges_in"), sem("x_in"), sem("bias_in"), sem("row_in")
        raw_in = [sem(f"raw_in{j}") for j in range(2)]
        raw_free = [sem(f"raw_free{j}") for j in range(2)]
        pad_done, consts, tiny_done = sem("pad_done"), sem("consts"), sem("tiny_done")
        step_d, dw_done, gt_done, vals_done, rng_done = (sem("dve_step"), sem("dw_done"), sem("gt_done"),
                                                         sem("vals_done"), sem("rng_done"))
        stats_done, var_done, std_done, norm_done = sem("stats_done"), sem("var_done"), sem("std_done"), sem("norm_done")
        h_done, ht_done, ht_hi, ht_lo = sem("h_done"), sem("ht_done"), sem("ht_hi_done"), sem("ht_lo_done")
        w_hi_done, w_lo_done, eye_added = sem("w_hi_done"), sem("w_lo_done"), sem("eye_added")
        pair_used = [sem(f"pair_used{m}") for m in range(4)]
        bias_ready, dots_done = sem("bias_ready"), sem("dots_done")
        prod_done, prod_hi, prod_lo, b_done = sem("prod_done"), sem("prod_hi"), sem("prod_lo"), sem("b_done")
        b_part = sem("b_part")
        stored = [sem(f"stored{m}") for m in range(KT)]
        cols_done, cols_out, cols_added = sem("cols_done"), sem("cols_out"), sem("cols_added")
        spread_done, rows_done = sem("spread_done"), sem("rows_done")
        hot_ready = [sem(f"hot_ready{j}") for j in range(J)]
        hot_free, win_done, win_free = sem("hot_free"), sem("win_done"), sem("win_free")
        logs_done, none_done, logs_ready = sem("logs_done"), sem("none_done"), sem("logs_ready")
        pool_turn, ranges_ready = sem("pool_turn"), sem("ranges_ready")
        logs_stored = [sem(f"logs_stored{s}") for s in range(2)]
        block = ctx.enter_context(nc.Block())

        def schedule():
            for hh in range(UNROLL):
                for i in range(WH):
                    yield hh * WH + i, hh, i

        TILES = UNROLL * WH // TILE_WINS
        SLOT_USES = (TILES + 1) // 2, TILES // 2

        def window_range(eng, w):
            first_group = eng.value_load(win_range[0:1, 0, bass.ds(w, 1)], min_val=0, max_val=G - 1)
            end = eng.value_load(win_range[0:1, 1, bass.ds(w, 1)], min_val=1, max_val=G)
            return first_group, end

        def slot_uses(rd, tile):
            return SLOT_USES[tile % 2] * rd + tile // 2

        def raw_uses(h, m):
            return (3, 2)[m % 2] * h + m // 2

        def pair_uses(h, m):
            return (2 * h + (m == SM)) if PAIR[m] == 1 else h

        def prods(h, kind, m):
            return 8 * h + (0 if kind == "M" else 4) + m

        @block.sync
        def _(sp):
            sp.dma_start(dst_i[:, :, :], io["dst"]).then_inc(edges_in, 16)
            sp.dma_start(src_i[:, :, :], io["src"]).then_inc(edges_in, 16)
            for n, name in enumerate(("bq", "bk", "bv", "bs")):
                sp.dma_start(bias[:, n, :], io[name]).then_inc(bias_in, 16)
            sp.dma_start(xs[:, 0:NT - 1, :], io["x"][0:(NT - 1) * P, :].rearrange("(t p) d -> p t d", p=P)
                         ).then_inc(x_in, 16)
            sp.wait_ge(pad_done, 1)
            sp.dma_start(xs[0:LAST, NT - 1, :], io["x"][(NT - 1) * P:N, :]).then_inc(x_in, 16)
            sp.dma_start(keep["s_row"][:, :], io["blin"].partition_broadcast(P)).then_inc(row_in, 16)
            for s in range(2):
                sp.sem_inc(logs_stored[s], 16)
            with sp.Fori(0, H // UNROLL) as rd:
                for wi, hh, i in schedule():
                    h = UNROLL * rd + hh
                    for m in SPLIT.get(i, ()):
                        sp.wait_ge(raw_free[m % 2], raw_uses(h, m) + 1)
                        sp.dma_start(raw[m % 2][:, :, :], io[NAMES[m]][bass.ds(h, 1)].rearrange(
                            "a p c n -> (a p) c n")).then_inc(raw_in[m % 2], 16)
                    if wi % TILE_WINS == TILE_WINS - 1:
                        tile = wi // TILE_WINS
                        t = TILES * rd + tile
                        sp.wait_ge(logs_ready, t + 2)
                        sp.dma_start(dram["L"][bass.ds(t, 1)].rearrange("a p n -> (a p) n"), logs[tile % 2][:, 0:N]
                                     ).then_inc(logs_stored[tile % 2], 16)
            for s in range(2):
                sp.wait_ge(logs_stored[s], 16 * SLOT_USES[s] * (H // UNROLL) + 16)

        @block.gpsimd
        def _(pool):
            for j in range(2):
                pool.sem_inc(raw_free[j], 1)
            nc.gpsimd.memset(xs[:, NT - 1, :], 0.0).then_inc(pad_done, 1)
            nc.gpsimd.memset(keep["ident"][:, :], 1.0).then_inc(pad_done, 1)
            pool.wait_ge(pad_done, 2)
            nc.gpsimd.affine_select(out=keep["ident"][:, :], in_=keep["ident"][:, :], compare_op=ALU.is_equal,
                                    fill=0.0, base=0, pattern=[[-1, P]], channel_multiplier=1).then_inc(consts, 1)
            nc.gpsimd.memset(ones[:, :], 1.0).then_inc(consts, 1)
            nc.gpsimd.memset(zero16[:, :], 0.0).then_inc(consts, 1)
            nc.gpsimd.memset(zero[:, :].bitcast(F32), 0.0).then_inc(consts, 1)

            def iota(out, pattern, base=0, step=0):
                nc.gpsimd.iota(out, pattern=pattern, base=base, channel_multiplier=step,
                               allow_small_or_imprecise_dtypes=True).then_inc(consts, 1)

            iota(win_i[:, :], [[1, NW]])
            iota(gup[:, :], [[0, 1]], 1, 1)
            iota(gdown[:, :], [[0, 1]], G, -1)
            iota(iota_key[:, :, :], [[0, J], [1, P]])
            iota(iota_col[:, :], [[1, SB]])
            iota(win_key[:, :], [[P, NW]])
            nc.gpsimd.memset(tiny[:, :], 2.0 ** -60).then_inc(tiny_done, 1)
            nc.gpsimd.memset(vs_cols[:, :], 0.0).then_inc(cols_added, 1)
            pool.wait_ge(vals_done, 1)
            nc.gpsimd.partition_all_reduce(rng[:, :, :].rearrange("p a w -> p (a w)"),
                                           vals[:, :, :].rearrange("p a w -> p (a w)"), G, RMAX).then_inc(rng_done, 1)
            pool.sem_inc(logs_ready, 1)
            with pool.Fori(0, H // UNROLL) as rd:
                for wi, hh, i in schedule():
                    h = UNROLL * rd + hh
                    for m in SPLIT.get(i, ()):
                        pool.wait_ge(w_hi_done, 5 * h + m + 1)
                        nc.gpsimd.tensor_tensor(w_lo[PAIR[m]][:, :, :], raw[m % 2][:, :, :],
                                                w_hi[PAIR[m]][:, :, :].bitcast(F32), ALU.subtract).then_inc(w_lo_done, 1)
                        pool.wait_ge(w_lo_done, 5 * h + m + 1)
                        pool.sem_inc(raw_free[m % 2], 1)
                    if wi % TILE_WINS == TILE_WINS - 1:
                        tile = wi // TILE_WINS
                        t = TILES * rd + tile
                        pool.wait_ge(logs_done, TILE_WINS * t + TILE_WINS)
                        pool.wait_ge(logs_ready, t + 1)
                        pool.sem_inc(pool_turn, 1)
                        now = logs[tile % 2][:, 0:N]
                        nc.gpsimd.tensor_scalar(none, now, -1.0, -BIG, ALU.is_lt, ALU.mult).then_inc(none_done, 1)
                        pool.wait_ge(none_done, t + 1)
                        nc.gpsimd.tensor_tensor(now, now, none, ALU.add).then_inc(logs_ready, 1)
                    if i == WH - 1:
                        pool.wait_ge(cols_out, 2 * h + 3)
                        nc.gpsimd.tensor_tensor(keep["uw"][:, :, bass.ds(h, 1)].rearrange("p c a -> p (c a)"),
                                                small[:, :, 0], small[:, :, 1], ALU.add).then_inc(cols_added, 1)
                        nc.gpsimd.tensor_tensor(small[:, :, 4], small[:, :, 2], small[:, :, 3], ALU.add
                                                ).then_inc(cols_added, 1)
                        pool.wait_ge(cols_added, 3 * h + 3)
                        nc.gpsimd.tensor_tensor(vs_cols[:, :], vs_cols[:, :], small[:, :, 4], ALU.add
                                                ).then_inc(cols_added, 1)
            for s in range(2):
                pool.wait_ge(logs_stored[s], 16 * SLOT_USES[s] * (H // UNROLL) + 16)
            pool.wait_ge(cols_added, 3 * H + 1)
            for i in range(2 * KT):
                nc.gpsimd.tensor_scalar(spread[:, i, :], ones[:, :], vs_cols[:, i:i + 1], None, ALU.mult
                                        ).then_inc(spread_done, 1)

        @block.scalar
        def _(act):
            def split_hi(h, m):
                act.wait_ge(raw_in[m % 2], 16 * raw_uses(h, m) + 16)
                act.wait_ge(pair_used[PAIR[m]], pair_uses(h, m) + 1)
                if m == LM:
                    act.wait_ge(eye_added, h + 1)
                nc.scalar.copy(w_hi[PAIR[m]][:, :, :], raw[m % 2][:, :, :]).then_inc(w_hi_done, 1)

            def store(n, m, to):
                act.wait_ge(prod_hi, n + 1)
                act.wait_ge(prod_lo, n + 3)
                act.dma_start(to(0)[:, m, :], o_hi[:, m, :].bitcast(F32)).then_inc(stored[m], 16)
                act.dma_start(to(1)[:, m, :], o_lo[:, m, :].bitcast(F32)).then_inc(stored[m], 16)

            def take_product(h, kind, m):
                n = prods(h, kind, m)
                act.wait_ge(prod_done, n + 1)
                act.wait_ge(stored[m], 8 * (n - m) + 32)
                nc.scalar.copy(o_hi[:, m, :], prod[m % 2][:, :]).then_inc(prod_hi, 1)

            act.sem_inc(win_free, 2)
            act.sem_inc(cols_out, 1)
            for m in range(KT):
                act.sem_inc(stored[m], 32)
                act.sem_inc(pair_used[m], 1)
            act.wait_ge(var_done, 1)
            nc.scalar.activation(std[:, :], std[:, :], ACT.Sqrt).then_inc(std_done, 1)
            act.wait_ge(norm_done, 1)
            for t in range(NT):
                nc.scalar.activation(xs[:, t, :], xs[:, t, :], ACT.Relu, bias=nmr[:, t:t + 1],
                                     scale=rstd[:, t:t + 1]).then_inc(h_done, 1)
                if t >= 1:
                    act.wait_ge(ht_done, t)
                    nc.scalar.copy(keep["hT_hi"][:, :, (t - 1) * P:t * P], hps[(t - 1) % 2]).then_inc(ht_hi, 1)
            act.wait_ge(ht_done, NT)
            nc.scalar.copy(keep["hT_hi"][:, :, (NT - 1) * P:NP], hps[(NT - 1) % 2]).then_inc(ht_hi, 1)
            act.wait_ge(tiny_done, 1)
            with act.Fori(0, H // UNROLL) as rd:
                pending = []
                for wi, hh, i in schedule():
                    h = UNROLL * rd + hh
                    for m in SPLIT.get(i, ()):
                        split_hi(h, m)
                    k, tile = wi % TILE_WINS, wi // TILE_WINS
                    w = UNROLL * WH * rd + wi
                    act.wait_ge(win_done, w + 1)
                    if k == 0:
                        act.wait_ge(logs_stored[tile % 2], 16 * slot_uses(rd, tile) + 16)
                    for a in range(TILE_WINS):
                        last = nc.scalar.activation(logs[tile % 2][k * WIN:(k + 1) * WIN, a * SB:(a + 1) * SB],
                                                    win[wi % 2][a * WIN:(a + 1) * WIN, :], ACT.Ln,
                                                    bias=tiny[a * WIN:(a + 1) * WIN, :])
                    last.then_inc(logs_done, 1)
                    act.wait_ge(logs_done, w + 1)
                    act.sem_inc(win_free, 1)
                    for kind, m in pending:
                        store(prods(h, kind, m), m, lambda half, kind=kind, h=h: dram[kind][
                            bass.ds(h, 1), half].rearrange("a p c n -> (a p) c n"))
                    pending = [(kind, m) for kind, m in WORK[i] if kind in "MA"]
                    for kind, m in WORK[i]:
                        if kind in "MA":
                            take_product(h, kind, m)
                        elif kind in ("uw", "vs"):
                            n = 2 * h + (kind == "vs")
                            act.wait_ge(cols_done, n + 1)
                            if kind == "uw":
                                act.wait_ge(cols_added, 3 * h + 1)
                            c = 0 if kind == "uw" else 2
                            nc.scalar.copy(small[:, :, c:c + 2], cols[:, :, c:c + 2]).then_inc(cols_out, 1)
            act.wait_ge(b_done, 1)
            for m in range(KT):
                act.wait_ge(stored[m], 16 * 4 * H + 32)
                nc.scalar.copy(o_hi[:, m, :], bps[m][:, :]).then_inc(prod_hi, 1)
                store(8 * H + m, m, lambda half: dram["B"][half])
            for m in range(KT):
                act.wait_ge(stored[m], 16 * 4 * H + 64)

        @block.vector
        def _(dve):
            count = [0]

            def step(ins):
                count[0] += 1
                ins.then_inc(step_d, 1)
                dve.wait_ge(step_d, count[0])

            dve.sem_inc(ht_lo, 2)
            dve.sem_inc(prod_lo, 2)
            dve.wait_ge(edges_in, 32)
            step(nc.vector.tensor_scalar(dw_i[:, :, :], dst_i[:, :, :], 5, None, ALU.arith_shift_right))
            nc.vector.tensor_copy(dwf[:, :, :], dw_i[:, :, :]).then_inc(dw_done, 1)
            nc.vector.tensor_copy(dstf[:, :, :], dst_i[:, :, :])
            step(nc.vector.tensor_copy(srcf[:, :, :], src_i[:, :, :]))
            step(nc.vector.tensor_scalar(blk[:, :, :], srcf[:, :, :], float(SB), None, ALU.is_ge))
            for a in (2, 3):
                step(nc.vector.scalar_tensor_tensor(out=blk[:, :, :], in0=srcf[:, :, :], scalar=float(a * SB),
                                                    in1=blk[:, :, :], op0=ALU.is_ge, op1=ALU.add))
            nc.vector.scalar_tensor_tensor(out=col[:, :, :], in0=blk[:, :, :], scalar=-float(SB),
                                           in1=srcf[:, :, :], op0=ALU.mult, op1=ALU.add)
            dve.wait_ge(dw_done, 1)
            step(nc.vector.scalar_tensor_tensor(out=dstf[:, :, :], in0=dwf[:, :, :], scalar=float(P - WIN),
                                                in1=dstf[:, :, :], op0=ALU.mult, op1=ALU.add))
            step(nc.vector.scalar_tensor_tensor(out=key[:, :, :], in0=blk[:, :, :], scalar=float(WIN),
                                                in1=dstf[:, :, :], op0=ALU.mult, op1=ALU.add))
            dve.wait_ge(gt_done, 1)
            for b in range(2):
                nc.vector.tensor_reduce(ends2[:, b, 0:1], gps[b], AX_X, ALU.min)
                last = nc.vector.tensor_reduce(ends2[:, b, 1:2], gps[b], AX_X, ALU.max)
            step(last)
            nc.vector.tensor_tensor(ends[:, 0:1], ends2[:, 0, 0:1], ends2[:, 1, 0:1], ALU.min)
            step(nc.vector.tensor_tensor(ends[:, 1:2], ends2[:, 0, 1:2], ends2[:, 1, 1:2], ALU.max))
            dve.wait_ge(consts, 10)
            step(nc.vector.tensor_scalar(flag0[:, :], win_i[:, :], ends[:, 0:1], None, ALU.is_ge))
            step(nc.vector.scalar_tensor_tensor(out=flag[:, :], in0=win_i[:, :], scalar=ends[:, 1:2],
                                                in1=flag0[:, :], op0=ALU.is_le, op1=ALU.mult))
            nc.vector.tensor_scalar(vals[:, 0, :], flag[:, :], gdown[:, :], None, ALU.mult)
            nc.vector.tensor_scalar(vals[:, 1, :], flag[:, :], gup[:, :], None, ALU.mult).then_inc(vals_done, 1)

            dve.wait_ge(bias_in, 64)
            step(nc.vector.tensor_copy(bias_r[:, :, :, 0], bias[:, :, :]))
            nc.vector.tensor_tensor(bias_r[:, :, :, 1], bias[:, :, :], bias_r[:, :, :, 0].bitcast(F32), ALU.subtract)
            step(nc.vector.tensor_tensor(bkq[:, :], bias[:, 0, :], bias[:, 1, :], ALU.mult))
            nc.vector.tensor_reduce(bkq4[:, :], bkq[:, :].rearrange("p (h c) -> p h c", h=H), AX_X,
                                    ALU.add).then_inc(bias_ready, 1)
            step(nc.vector.memset(first[:, :], 0.0))
            step(nc.vector.memset(first[:, 0:1], 1.0))

            dve.wait_ge(x_in, 32)
            with dve.Fori(0, NT) as t:
                nc.vector.bn_stats(stats[:, bass.ds(t, 1), :].rearrange("p a b -> p (a b)"),
                                   xs[:, bass.ds(t, 1), :].rearrange("p a b -> p (a b)")).then_inc(stats_done, 1)
            dve.wait_ge(stats_done, NT)
            for t in range(NT):
                last = nc.vector.bn_aggr(mv[:, t, :], stats[:, t, :])
            step(last)
            nc.vector.tensor_scalar(std[:, :], mv[:, :, 1], EPS, None, ALU.add).then_inc(var_done, 1)
            dve.wait_ge(std_done, 1)
            step(nc.vector.reciprocal(rstd[:, :], std[:, :]))
            nc.vector.scalar_tensor_tensor(out=nmr[:, :], in0=mv[:, :, 0], scalar=-1.0, in1=rstd[:, :],
                                           op0=ALU.mult, op1=ALU.mult).then_inc(norm_done, 1)

            dve.wait_ge(rng_done, 1)
            step(nc.vector.tensor_scalar(rlo[:, :], rng[0:1, 0, :], -1.0, float(G), ALU.mult, ALU.add))
            step(nc.vector.tensor_scalar(rlo[:, :], rlo[:, :], float(G - 1), None, ALU.min))
            step(nc.vector.scalar_tensor_tensor(out=rhi[:, :], in0=rlo[:, :], scalar=1.0, in1=rng[0:1, 1, :],
                                                op0=ALU.add, op1=ALU.max))
            nc.vector.tensor_copy(win_range[:, 0, :], rlo[:, :])
            nc.vector.tensor_copy(win_range[:, 1, :], rhi[:, :]).then_inc(ranges_ready, 1)
            dve.wait_ge(dots_done, 1)
            nc.vector.tensor_copy(keep["bqbk"][:, :], dots)

            for t in range(NT):
                dve.wait_ge(ht_hi, t + 1)
                nc.vector.tensor_tensor(keep["hT_lo"][:, :, t * P:(t + 1) * P], hps[t % 2],
                                        keep["hT_hi"][:, :, t * P:(t + 1) * P].bitcast(F32),
                                        ALU.subtract).then_inc(ht_lo, 1)
            dve.wait_ge(ranges_ready, 1)
            turn = dve.alloc_register("dve_turn")
            dve.reg_mov(turn, 1)
            with dve.Fori(0, H // UNROLL) as rd:
                pending = []
                for wi, hh, i in schedule():
                    h = UNROLL * rd + hh
                    w = UNROLL * WH * rd + wi
                    if i == 2:
                        dve.wait_ge(raw_in[LM % 2], 16 * raw_uses(h, LM) + 16)
                        for c in range(KT):
                            d = raw[LM % 2][:, c, c * P:(c + 1) * P]
                            last = nc.vector.scalar_tensor_tensor(out=d, in0=keep["ident"][:, :],
                                                                  scalar=first[:, bass.ds(h, 1)], in1=d,
                                                                  op0=ALU.mult, op1=ALU.add)
                        last.then_inc(eye_added, 1)
                    lo, end = window_range(dve, w)
                    with dve.Fori(lo, end) as g:
                        n = dve.snap(turn, min_val=1, max_val=MOST_GROUPS)
                        slot = bass.ds(n % SLOTS, 1)
                        dve.wait_ge(hot_free, n)
                        nc.vector.scalar_tensor_tensor(
                            out=hot_key[:, slot].rearrange("p a j c -> p (a j) c"), in0=iota_key[:, :, :],
                            scalar=win_key[:, bass.ds(w, 1)], in1=key[:, :, bass.ds(g, 1)].broadcast_to([EP, J, P]),
                            op0=ALU.add, op1=ALU.is_equal)
                        for j in range(J):
                            nc.vector.tensor_scalar(hot_col[:, slot, j].rearrange("p a c -> p (a c)"), iota_col[:, :],
                                                    col[:, j, bass.ds(g, 1)], None, ALU.is_equal
                                                    ).then_inc(hot_ready[j], 1)
                        dve.reg_add(turn, turn, 1)
                    for kind, m in pending:
                        dve.wait_ge(prod_hi, prods(h, kind, m) + 1)
                        nc.vector.tensor_tensor(o_lo[:, m, :], prod[m % 2][:, :], o_hi[:, m, :].bitcast(F32),
                                                ALU.subtract).then_inc(prod_lo, 1)
                    pending = [(kind, m) for kind, m in WORK[i] if kind in "MA"]
            dve.wait_ge(b_done, 1)
            for m in range(KT):
                dve.wait_ge(prod_hi, 8 * H + m + 1)
                nc.vector.tensor_tensor(o_lo[:, m, :], bps[m][:, :], o_hi[:, m, :].bitcast(F32),
                                        ALU.subtract).then_inc(prod_lo, 1)
            dve.wait_ge(rows_done, 1)
            dve.wait_ge(row_in, 16)
            nc.vector.tensor_copy(keep["v_row"][:, :], prod[0][:, :])
            nc.vector.tensor_tensor(keep["s_row"][:, :], prod[1][:, :], keep["s_row"][:, :], ALU.add)

        @block.tensor
        def _(pe):
            def product(out, a, b, m, start, stop):
                a, b = PAIR[a], PAIR[b]
                for c in range(KT):
                    last = three(nc, out, w_hi[a][:, c, m * P:(m + 1) * P], w_lo[a][:, c, m * P:(m + 1) * P],
                                 w_hi[b][:, c, :], w_lo[b][:, c, :], start and c == 0, stop and c == KT - 1)
                return last

            def column(row, at, matrix, m, kind, h):
                for c in range(KT):
                    for half, w in enumerate((w_hi, w_lo)):
                        rhs = bias_r[:, kind, bass.ds(h * KT + c, 1), :].rearrange("p a b -> p (a b)")
                        last = nc.tensor.matmul(cols[:, row, at:at + 2], w[PAIR[matrix]][:, c, m * P:(m + 1) * P], rhs,
                                                start=(c == 0 and half == 0), stop=(c == KT - 1 and half == 1),
                                                skip_group_check=True)
                return last

            def work(h, w, kind, m):
                if kind in "MA":
                    a, b = (QM, KM) if kind == "M" else (VM, LM)
                    if m == 0:
                        pe.wait_ge(w_lo_done, 5 * h + b + 1)
                    pe.wait_ge(prod_lo, prods(h, kind, m) + 1)
                    product(prod[m % 2][:, :], a, b, m, True, True).then_inc(prod_done, 1)
                    if m == KT - 1:
                        pe.wait_ge(prod_done, prods(h, kind, m) + 1)
                        for matrix in (QM, KM) if kind == "M" else (VM,):
                            pe.sem_inc(pair_used[PAIR[matrix]], 1)
                elif kind == "B":
                    if m == 0:
                        pe.wait_ge(w_lo_done, 5 * h + SM + 1)
                    last = product(bps[m][:, :], SM, LM, m, False, False)
                    if m == KT - 1:
                        last.then_inc(b_part, 1)
                        pe.wait_ge(b_part, h + 1)
                        for matrix in (SM, LM):
                            pe.sem_inc(pair_used[PAIR[matrix]], 1)
                else:
                    pe.wait_ge(win_free, w + 2)
                    at, (a, b), kinds = (0, (KM, QM), (0, 1)) if kind == "uw" else (2, (LM, LM), (2, 3))
                    for m in range(KT):
                        column(m, at, a, m, kinds[0], h)
                        last = column(KT + m, at, b, m, kinds[1], h)
                    last.then_inc(cols_done, 1)

            pe.sem_inc(hot_free, SLOTS)
            pe.wait_ge(consts, 4)
            pe.wait_ge(dw_done, 1)
            for j in range(J):
                out = gps[j // 3][:, (j % 3) * EP:(j % 3 + 1) * EP]
                last = nc.tensor.transpose(out, dwf[:, j, :], keep["ident"][0:EP, 0:EP])
            last.then_inc(gt_done, 1)
            pe.wait_ge(bias_ready, 1)
            nc.tensor.matmul(dots, ones[:, :], bkq4[:, :], start=True, stop=True).then_inc(dots_done, 1)
            for t in range(NT):
                pe.wait_ge(h_done, t + 1)
                pe.wait_ge(ht_lo, t + 1)
                for c in range(KT):
                    last = nc.tensor.transpose(hps[t % 2][:, c, :], xs[:, t, c * P:(c + 1) * P], keep["ident"][:, :])
                last.then_inc(ht_done, 1)
            pe.wait_ge(ht_lo, NT + 2)
            pe.wait_ge(ranges_ready, 1)
            for m in range(KT):
                nc.tensor.matmul(bps[m][:, :], zero[:, 0:P], zero[:, :], start=True, stop=False, skip_group_check=True)
            turn = pe.alloc_register("pe_turn")
            pe.reg_mov(turn, 1)
            with pe.Fori(0, H // UNROLL) as rd:
                for wi, hh, i in schedule():
                    h = UNROLL * rd + hh
                    w = UNROLL * WH * rd + wi
                    lo, end = window_range(pe, w)
                    pe.wait_ge(win_free, w + 1)
                    if i in (0, 4):
                        pe.wait_ge(cols_out, 2 * h + 1 + (i == 4))
                    nc.tensor.matmul(win[wi % 2], zero16[:, 0:P], zero16[:, 0:SB], start=True, stop=False,
                                     skip_group_check=True)
                    with pe.Fori(lo, end):
                        n = pe.snap(turn, min_val=1, max_val=MOST_GROUPS)
                        slot = bass.ds(n % SLOTS, 1)
                        for j in range(J):
                            pe.wait_ge(hot_ready[j], n)
                            last = nc.tensor.matmul(win[wi % 2], hot_key[:, slot, j].rearrange("p a c -> p (a c)"),
                                                    hot_col[:, slot, j].rearrange("p a c -> p (a c)"),
                                                    start=False, stop=False, skip_group_check=True)
                        last.then_inc(hot_free, 1)
                        pe.reg_add(turn, turn, 1)
                    nc.tensor.matmul(win[wi % 2], zero16[:, 0:P], zero16[:, 0:SB], start=False, stop=True,
                                     skip_group_check=True).then_inc(win_done, 1)
                    for kind, m in WORK[i]:
                        work(h, w, kind, m)
            for m in range(KT):
                last = nc.tensor.matmul(bps[m][:, :], zero[:, 0:P], zero[:, :], start=False, stop=True,
                                        skip_group_check=True)
            last.then_inc(b_done, 1)
            pe.wait_ge(spread_done, 2 * KT)
            pe.wait_ge(prod_lo, 8 * H + 2)
            for n in range(2):
                for m in range(KT):
                    last = nc.tensor.matmul(prod[n][:, m * P:(m + 1) * P], spread[:, n * KT + m, :],
                                            keep["ident"][:, :], start=True, stop=True)
            last.then_inc(rows_done, 1)


def attend(nc, io, keep, dram, sem):
    with ExitStack() as ctx:
        sb = lambda name, shape, dt: ctx.enter_context(nc.sbuf_tensor(name, shape, dt))
        m_r = [sb(f"m_{x}", [P, KT, D], F32R) for x in ("hi", "lo")]
        a_r = [sb(f"a_{x}", [P, KT, D], F32R) for x in ("hi", "lo")]
        g_r = [sb(f"g_{x}", [P, NT, D], F32R) for x in ("hi", "lo")]
        qt_r = [sb(f"qt_{x}", [P, KT, P], F32R) for x in ("hi", "lo")]
        pt_r = [sb(f"pt_{x}", [P, NT, P], F32R) for x in ("hi", "lo")]
        q = sb("q", [P, KT, NP], F32)
        y = sb("y", [P, NT, D], F32)
        probs = sb("probs", [P, N], F32)
        logs = sb("logs_in", [P, N], F32)
        w_r = sb("w_r", [P, KT, 2, H], F32R)
        r = sb("r", [P, H * NT], F32)
        r2 = sb("r2", [P, NT, 2 * H], F32)
        r3 = sb("r3", [P, NT, H], F32)
        has = sb("has", [P, NT], F32)
        u = sb("u", [P, KT], F32)
        mx, amax, shift, den, total, share = (sb(x, [P, 1], F32) for x in ("mx", "amax", "shift", "den", "total", "share"))
        gamma = sb("gamma", [P, D], F32)
        beta = sb("beta", [P, D], F32)
        stats = sb("stats2", [P, NT, 6], F32)
        mv = sb("mv2", [P, NT, 2], F32)
        std = sb("std2", [P, NT], F32)
        rstd = sb("rstd2", [P, NT], F32)
        nmr = sb("nmr2", [P, NT], F32)
        x = q[:, :, :].rearrange("p c n -> p (c n)").rearrange("p (t d) -> p t d", t=NT)
        h_r = (keep["hT_hi"], keep["hT_lo"])

        sps = ctx.enter_context(nc.psum_tensor("sps", [P, 3 * 512], F32))
        tps = [ctx.enter_context(nc.psum_tensor(f"tps{g}", [P, 4, P], F32)) for g in range(len(TG))]
        wps = [ctx.enter_context(nc.psum_tensor(f"wps{b}", [P, 512], F32)) for b in range(2)]

        m_in, a_in, logs_in, row_in, x_in = sem("m_in"), sem("a_in"), sem("logs_arrived"), sem("row_in2"), sem("x_in2")
        m_used, a_used, logs_used = sem("m_used"), sem("a_used"), sem("logs_used")
        w_done = [sem(f"w_done{b}") for b in range(2)]
        w_free = [sem(f"w_free{b}") for b in range(2)]
        q_done, qt_hi, qt_lo, g_hi, g_lo = sem("q_done"), sem("qt_hi_done"), sem("qt_lo_done"), sem("g_hi_done"), sem("g_lo_done")
        s_done, shift_done, exp_done = sem("s_done"), sem("shift_done"), sem("exp_done")
        t_done, pt_hi, pt_lo, y_done = sem("t_done"), sem("pt_hi_done"), sem("pt_lo_done"), sem("y_done")
        w_r_done, r_done, r_ready = sem("w_r_done"), sem("r_done"), sem("r_ready")
        chain, mx_done, amax_done, total_done, share_done = (sem("chain"), sem("mx_done"), sem("amax_done"),
                                                           sem("total_done"), sem("share_done"))
        u_done, row_turn = sem("u_done"), sem("row_turn")
        st_done, mv_done, yb_done = sem("st_done"), sem("mv_done"), sem("yb_done")
        var_done, std_done, norm_ready = sem("var_done"), sem("std_done2"), sem("norm_ready")
        z_done, zg_done, xb_done, out_ready, out_stored = (sem("z_done"), sem("zg_done"), sem("xb_done"),
                                                           sem("out_ready"), sem("out_stored"))
        block = ctx.enter_context(nc.Block())
        W0, W1, START = 11 + NT, 11, NT // 2

        def use(h, i):
            return START + (W0, W1)[i % 2] * h + i // 2

        def use_pv(h, t):
            return START + W0 * h + 11 + t

        @block.sync
        def _(sp):
            sp.dma_start(gamma[:, :], io["gamma"].partition_broadcast(P)).then_inc(row_in, 16)
            sp.dma_start(beta[:, :], io["beta"].partition_broadcast(P)).then_inc(row_in, 16)
            with sp.Fori(0, H) as h:
                with sp.Fori(0, NT) as t:
                    sp.wait_ge(logs_used, NT * h + t + 1)
                    sp.dma_start(logs[:, :], dram["L"][bass.ds(t, 1)].rearrange("a p n -> (a p) n")
                                 ).then_inc(logs_in, 16)
            sp.wait_ge(s_done, H * NT + 1)
            sp.dma_start(x[:, 0:NT - 1, :], io["x"][0:(NT - 1) * P, :].rearrange("(t p) d -> p t d", p=P)
                         ).then_inc(x_in, 16)
            sp.dma_start(x[0:LAST, NT - 1, :], io["x"][(NT - 1) * P:N, :]).then_inc(x_in, 16)
            with sp.Fori(0, NT - 1) as t:
                sp.wait_ge(out_ready, t + 1)
                sp.dma_start(io["out"][bass.ds(t * P, P), :], y[:, bass.ds(t, 1), :].rearrange("p a d -> p (a d)")
                             ).then_inc(out_stored, 16)
            sp.wait_ge(out_ready, NT)
            sp.dma_start(io["out"][(NT - 1) * P:N, :], y[0:LAST, NT - 1, :]).then_inc(out_stored, 16)
            sp.wait_ge(out_stored, 16 * NT)

        @block.gpsimd
        def _(pool):
            for half in range(2):
                pool.dma_start(a_r[half][:, :, :].bitcast(F32), dram["B"][half]).then_inc(a_in, 16)
            for h in range(H):
                pool.wait_ge(m_used, h + 1)
                for half in range(2):
                    pool.dma_start(m_r[half][:, :, :].bitcast(F32), dram["M"][h, half]).then_inc(m_in, 16)
                pool.wait_ge(a_used, h + 1)
                for half in range(2):
                    pool.dma_start(a_r[half][:, :, :].bitcast(F32), dram["A"][h, half]).then_inc(a_in, 16)
            pool.wait_ge(x_in, 32)
            pool.wait_ge(row_in, 32)
            for t in range(NT):
                p = rows_of(t)
                nc.gpsimd.tensor_tensor(x[0:p, t, :], x[0:p, t, :], beta[0:p, :], ALU.add).then_inc(xb_done, 1)

        @block.tensor
        def _(pe):
            def scores(c, n):
                a, b = CH_N[c]
                for k in range(KT):
                    last = three(nc, sps[:, a:b], qt_r[0][:, k, :], qt_r[1][:, k, :], h_r[0][:, k, a:b],
                                 h_r[1][:, k, a:b], k == 0, k == KT - 1)
                if c == len(CH_N) - 1:
                    last.then_inc(s_done, 1)

            def transposes(g, n):
                pe.wait_ge(pt_lo, 3 * n + g + 1)
                a, b = TG[g]
                for s in range(a, b):
                    last = nc.tensor.transpose(tps[g][0:rows_of(s), s - a, :], probs[:, s * P:s * P + rows_of(s)],
                                               keep["ident"][:, :])
                last.then_inc(t_done, 1)

            def apply(h, t, n):
                pe.wait_ge(w_free[0], use_pv(h, t) + 1)
                pe.wait_ge(g_lo, NT * h + NT)
                for g, (a, b) in enumerate(TG):
                    pe.wait_ge(pt_lo, 3 * n + g + 4)
                    for s in range(a, b):
                        p = rows_of(s)
                        last = three(nc, wps[0][:, :], pt_r[0][0:p, s, :], pt_r[1][0:p, s, :], g_r[0][0:p, s, :],
                                     g_r[1][0:p, s, :], s == 0, s == NT - 1)
                last.then_inc(w_done[0], 1)

            def rows_times(s, i, before):
                b = i % 2
                pe.wait_ge(w_free[b], before + 1)
                for k in range(KT):
                    last = three(nc, wps[b][:, :], h_r[0][:, k, s * P:(s + 1) * P], h_r[1][:, k, s * P:(s + 1) * P],
                                 a_r[0][:, k, :], a_r[1][:, k, :], k == 0, k == KT - 1)
                last.then_inc(w_done[b], 1)

            pe.sem_inc(m_used, 1)
            pe.sem_inc(s_done, 1)
            pe.wait_ge(w_r_done, 1)
            for s in range(NT):
                for k in range(KT):
                    for half in range(2):
                        last = nc.tensor.matmul(sps[:, s * 8:s * 8 + 8], h_r[half][:, k, s * P:(s + 1) * P],
                                                w_r[:, k, :, :].rearrange("p a h -> p (a h)"),
                                                start=(k == 0 and half == 0), stop=(k == KT - 1 and half == 1))
            last.then_inc(r_done, 1)
            pe.wait_ge(a_in, 32)
            for s in range(NT):
                rows_times(s, s, s // 2)
            pe.wait_ge(w_done[1], START)
            pe.sem_inc(a_used, 1)
            pe.wait_ge(r_ready, 1)
            with pe.Fori(0, H) as h:
                pe.wait_ge(m_in, 32 * h + 32)
                for m in range(KT):
                    for c, (a, b) in enumerate(CH_NP):
                        i = 3 * m + c
                        pe.wait_ge(w_free[i % 2], use(h, i) + 1)
                        for k in range(KT):
                            last = three(nc, wps[i % 2][:, 0:b - a], m_r[0][:, k, m * P:(m + 1) * P],
                                         m_r[1][:, k, m * P:(m + 1) * P], h_r[0][:, k, a:b], h_r[1][:, k, a:b],
                                         k == 0, k == KT - 1)
                        last.then_inc(w_done[i % 2], 1)
                pe.wait_ge(w_done[1], use(h, 11) + 1)
                pe.sem_inc(m_used, 1)
                pe.wait_ge(a_in, 32 * h + 64)
                for s in range(NT // 2):
                    rows_times(s, 12 + s, use(h, 12 + s))
                pe.wait_ge(qt_lo, NT * h + 1)
                for c in range(len(CH_N)):
                    scores(c, NT * h)
                for s in range(NT // 2, NT):
                    rows_times(s, 12 + s, use(h, 12 + s))
                pe.wait_ge(w_done[1], use(h, 21) + 1)
                pe.sem_inc(a_used, 1)
                with pe.Fori(0, NT - 1) as t:
                    n = NT * h + t
                    pe.wait_ge(exp_done, n + 1)
                    for g in range(len(TG)):
                        transposes(g, n)
                        if g == 0:
                            pe.wait_ge(qt_lo, n + 2)
                        scores(g, n + 1)
                    apply(h, t, n)
                n = NT * h + NT - 1
                pe.wait_ge(exp_done, n + 1)
                for g in range(len(TG)):
                    transposes(g, n)
                apply(h, NT - 1, n)

        @block.scalar
        def _(act):
            def q_hi(h, t, n):
                act.wait_ge(s_done, n + 1)
                nc.scalar.copy(qt_r[0][:, :, :], q[:, :, bass.ds(t * P, P)]).then_inc(qt_hi, 1)

            def softmax(n):
                act.wait_ge(shift_done, n + 1)
                nc.scalar.activation(probs[:, :], sps[:, 0:N], ACT.Exp, bias=shift[:, :],
                                     accum_out=den[:, :]).then_inc(exp_done, 1)

            def take_g(h, s):
                i = 12 + s
                act.wait_ge(w_done[i % 2], use(h, i) + 1)
                nc.scalar.copy(g_r[0][:, s, :], wps[i % 2][:, :]).then_inc(g_hi, 1)

            def take_pt(n):
                for g, (a, b) in enumerate(TG):
                    act.wait_ge(t_done, 3 * n + g + 1)
                    whole = [s for s in range(a, b) if rows_of(s) == P]
                    z = a + len(whole)
                    last = nc.scalar.copy(pt_r[0][:, a:z, :], tps[g][:, 0:z - a, :])
                    if z < b:
                        last = nc.scalar.copy(pt_r[0][0:LAST, z, :], tps[g][0:LAST, z - a, :])
                    last.then_inc(pt_hi, 1)

            act.sem_inc(w_free[0], 1)
            act.sem_inc(w_free[1], 1)
            with act.Fori(0, H) as h:
                nc.scalar.mul(u[:, :], keep["uw"][:, 0:KT, bass.ds(h, 1)].rearrange("p c a -> p (c a)"), SCALE
                              ).then_inc(u_done, 1)
                act.wait_ge(u_done, h + 1)
                for m in range(KT):
                    for c, (a, b) in enumerate(CH_NP):
                        i = 3 * m + c
                        act.wait_ge(w_done[i % 2], use(h, i) + 1)
                        nc.scalar.activation(q[:, m, a:b], wps[i % 2][:, 0:b - a], ACT.Identity,
                                             bias=u[:, m:m + 1], scale=SCALE).then_inc(w_free[i % 2], 1)
                act.wait_ge(w_free[0], use(h, 10) + 2)
                act.wait_ge(w_free[1], use(h, 11) + 2)
                q_hi(h, 0, NT * h)
                for s in range(NT // 2):
                    take_g(h, s)
                q_hi(h, 1, NT * h + 1)
                take_g(h, NT // 2)
                softmax(NT * h)
                for s in range(NT // 2 + 1, NT):
                    take_g(h, s)
                with act.Fori(0, NT - 2) as t:
                    n = NT * h + t
                    take_pt(n)
                    q_hi(h, t + 2, n + 2)
                    softmax(n + 1)
                n = NT * h + NT - 2
                take_pt(n)
                softmax(n + 1)
                take_pt(n + 1)
            act.wait_ge(var_done, 1)
            nc.scalar.activation(std[:, :], std[:, :], ACT.Sqrt).then_inc(std_done, 1)
            act.wait_ge(norm_ready, 1)
            for t in range(NT):
                nc.scalar.activation(y[:, t, :], y[:, t, :], ACT.Identity, bias=nmr[:, t:t + 1],
                                     scale=rstd[:, t:t + 1]).then_inc(z_done, 1)

        @block.vector
        def _(dve):
            def q_lo(t, n):
                dve.wait_ge(qt_hi, n + 1)
                nc.vector.tensor_tensor(qt_r[1][:, :, :], q[:, :, bass.ds(t * P, P)], qt_r[0][:, :, :].bitcast(F32),
                                        ALU.subtract).then_inc(qt_lo, 1)

            def row_max(n):
                dve.wait_ge(share_done, n + 1)
                dve.wait_ge(s_done, n + 2)
                dve.wait_ge(logs_in, 16 * n + 16)
                dve.sem_inc(row_turn, 1)
                nc.vector.tensor_tensor_reduce(sps[:, 0:N], sps[:, 0:N], logs[:, :], 1.0, -BIG / 2, ALU.add, ALU.max,
                                               mx[:, :]).then_inc(mx_done, 1)
                dve.wait_ge(mx_done, n + 1)
                dve.sem_inc(logs_used, 1)
                nc.vector.tensor_scalar(amax[:, :], mx[:, :], r[:, bass.ds(n, 1)], None, ALU.add
                                        ).then_inc(amax_done, 1)
                dve.wait_ge(amax_done, n + 1)
                nc.vector.tensor_tensor(shift[:, :], r[:, bass.ds(n, 1)], amax[:, :], ALU.subtract).then_inc(shift_done, 1)

            def split_g(h, s):
                i = 12 + s
                dve.wait_ge(g_hi, NT * h + s + 1)
                nc.vector.tensor_tensor(g_r[1][:, s, :], wps[i % 2][:, :], g_r[0][:, s, :].bitcast(F32),
                                        ALU.subtract).then_inc(w_free[i % 2], 1)
                if s == NT - 1:
                    dve.wait_ge(w_free[1], use(h, 21) + 2)
                    dve.sem_inc(g_lo, NT)

            def split_pt(n):
                for g, (a, b) in enumerate(TG):
                    dve.wait_ge(pt_hi, 3 * n + g + 1)
                    z = a + len([s for s in range(a, b) if rows_of(s) == P])
                    last = nc.vector.tensor_tensor(pt_r[1][:, a:z, :], tps[g][:, 0:z - a, :],
                                                   pt_r[0][:, a:z, :].bitcast(F32), ALU.subtract)
                    if z < b:
                        last = nc.vector.tensor_tensor(pt_r[1][0:LAST, z, :], tps[g][0:LAST, z - a, :],
                                                       pt_r[0][0:LAST, z, :].bitcast(F32), ALU.subtract)
                    last.then_inc(pt_lo, 1)

            def take_share(t, n):
                dve.wait_ge(exp_done, n + 1)
                nc.vector.tensor_scalar(has[:, bass.ds(t, 1)], den[:, :], 0.0, None, ALU.is_gt)
                nc.vector.tensor_scalar(total[:, :], den[:, :], 2.0 ** -60, None, ALU.max).then_inc(total_done, 1)
                dve.wait_ge(total_done, n + 1)
                nc.vector.reciprocal(share[:, :], total[:, :]).then_inc(share_done, 1)

            def add_head(h, t, n):
                dve.wait_ge(share_done, n + 2)
                dve.wait_ge(w_done[0], use_pv(h, t) + 1)
                yt = y[:, bass.ds(t, 1), :].rearrange("p a d -> p (a d)")
                nc.vector.scalar_tensor_tensor(out=yt, in0=wps[0][:, :], scalar=share[:, :], in1=yt, op0=ALU.mult,
                                               op1=ALU.add).then_inc(w_free[0], 1)

            count = [0]

            def step(ins):
                count[0] += 1
                ins.then_inc(chain, 1)
                dve.wait_ge(chain, count[0])

            dve.sem_inc(pt_lo, 3)
            dve.sem_inc(logs_used, 1)
            dve.sem_inc(share_done, 1)
            w = keep["uw"][:, KT:2 * KT, :]
            step(nc.vector.tensor_copy(w_r[:, :, 0, :], w))
            nc.vector.tensor_tensor(w_r[:, :, 1, :], w, w_r[:, :, 0, :].bitcast(F32), ALU.subtract).then_inc(w_r_done, 1)
            dve.wait_ge(r_done, 1)
            step(nc.vector.tensor_copy(r2[:, :, :], sps[:, 0:8 * NT].rearrange("p (t a) -> p t a", t=NT)))
            step(nc.vector.tensor_tensor(r3[:, :, :], r2[:, :, 0:H], r2[:, :, H:2 * H], ALU.add))
            for h in range(H):
                last = nc.vector.tensor_scalar(r[:, h * NT:(h + 1) * NT], r3[:, :, h], keep["bqbk"][:, h:h + 1], SCALE,
                                               ALU.add, ALU.mult)
            last.then_inc(r_ready, 1)
            dve.wait_ge(r_ready, 1)
            for s in range(NT):
                dve.wait_ge(w_done[s % 2], s // 2 + 1)
                last = nc.vector.tensor_tensor(y[:, s, :], wps[s % 2][:, :], keep["s_row"][:, :], ALU.add)
                last.then_inc(w_free[s % 2], 1)
            with dve.Fori(0, H) as h:
                q_lo(0, NT * h)
                for s in range(NT // 2):
                    split_g(h, s)
                row_max(NT * h)
                q_lo(1, NT * h + 1)
                for s in range(NT // 2, NT):
                    split_g(h, s)
                with dve.Fori(0, NT - 2) as t:
                    n = NT * h + t
                    take_share(t, n)
                    split_pt(n)
                    row_max(n + 1)
                    q_lo(t + 2, n + 2)
                    add_head(h, t, n)
                n = NT * h + NT - 2
                take_share(NT - 2, n)
                split_pt(n)
                row_max(n + 1)
                add_head(h, NT - 2, n)
                take_share(NT - 1, n + 1)
                split_pt(n + 1)
                add_head(h, NT - 1, n + 1)
            dve.wait_ge(w_free[0], START + W0 * H + 1)
            with dve.Fori(0, NT) as t:
                yt = y[:, bass.ds(t, 1), :].rearrange("p a d -> p (a d)")
                nc.vector.scalar_tensor_tensor(out=yt, in0=keep["v_row"][:, :], scalar=has[:, bass.ds(t, 1)], in1=yt,
                                               op0=ALU.mult, op1=ALU.add).then_inc(yb_done, 1)
                dve.wait_ge(yb_done, t + 1)
                nc.vector.bn_stats(stats[:, bass.ds(t, 1), :].rearrange("p a b -> p (a b)"), yt).then_inc(st_done, 1)
            dve.wait_ge(st_done, NT)
            for t in range(NT):
                last = nc.vector.bn_aggr(mv[:, t, :], stats[:, t, :])
            last.then_inc(mv_done, 1)
            dve.wait_ge(mv_done, 1)
            nc.vector.tensor_scalar(std[:, :], mv[:, :, 1], EPS, None, ALU.add).then_inc(var_done, 1)
            dve.wait_ge(std_done, 1)
            step(nc.vector.reciprocal(rstd[:, :], std[:, :]))
            nc.vector.scalar_tensor_tensor(out=nmr[:, :], in0=mv[:, :, 0], scalar=-1.0, in1=rstd[:, :], op0=ALU.mult,
                                           op1=ALU.mult).then_inc(norm_ready, 1)
            dve.wait_ge(row_in, 32)
            for t in range(NT):
                p = rows_of(t)
                dve.wait_ge(z_done, t + 1)
                nc.vector.tensor_tensor(y[0:p, t, :], y[0:p, t, :], gamma[0:p, :], ALU.mult).then_inc(zg_done, 1)
                dve.wait_ge(zg_done, t + 1)
                dve.wait_ge(xb_done, t + 1)
                nc.vector.tensor_tensor(y[0:p, t, :], y[0:p, t, :], x[0:p, t, :], ALU.add).then_inc(out_ready, 1)


def build(nc, io):
    with ExitStack() as ctx:
        keep_sb = lambda name, shape, dt: ctx.enter_context(nc.sbuf_tensor(name, shape, dt))
        sem = lambda name: ctx.enter_context(nc.semaphore(name))
        keep = {
            "hT_hi": keep_sb("hT_hi", [P, KT, NP], F32R),
            "hT_lo": keep_sb("hT_lo", [P, KT, NP], F32R),
            "ident": keep_sb("ident", [P, P], F32),
            "uw": keep_sb("uw", [P, 2 * KT, H], F32),
            "bqbk": keep_sb("bqbk", [P, H], F32),
            "v_row": keep_sb("v_row", [P, D], F32),
            "s_row": keep_sb("s_row", [P, D], F32),
        }
        r32 = lambda name, shape: nc.dram_tensor(name, shape, F32).ap()
        dram = {
            "M": r32("M_parts", [H, 2, P, KT, D]),
            "A": r32("A_parts", [H, 2, P, KT, D]),
            "B": r32("B_parts", [2, P, KT, D]),
            "L": nc.dram_tensor("log_counts", [NT, P, N], F32).ap(),
        }
        with ExitStack() as sems:
            fold_and_count(nc, io, keep, dram, lambda name: sems.enter_context(nc.semaphore(name)))
        attend(nc, io, keep, dram, sem)


def kernel(x, src, dst, L0_gnn_Wq, L0_gnn_bq, L0_gnn_Wk, L0_gnn_bk, L0_gnn_Wv, L0_gnn_bv, L0_gnn_Wskip, L0_gnn_bskip,
           L0_gnn_Wlin, L0_gnn_blin, L0_gnn_gamma, L0_gnn_beta):
    import numpy as np
    import concourse.bacc as bacc
    from concourse.bass_utils import run_bass_kernel_spmd

    tiled = lambda w: np.ascontiguousarray(np.asarray(w).reshape(H, KT, P, D).transpose(0, 2, 1, 3))
    edges = lambda e: np.ascontiguousarray(np.asarray(e).reshape(G, J, EP).transpose(2, 1, 0))
    column = lambda b: np.ascontiguousarray(np.asarray(b).reshape(H * KT, P).T)
    arrays = {
        "x": np.ascontiguousarray(x), "src": edges(src), "dst": edges(dst),
        "Wq": tiled(np.asarray(L0_gnn_Wq).T), "Wk": tiled(np.asarray(L0_gnn_Wk).T),
        "Wv": tiled(np.asarray(L0_gnn_Wv).T), "Ws": tiled(np.asarray(L0_gnn_Wskip).T), "Wl": tiled(L0_gnn_Wlin),
        "bq": column(L0_gnn_bq), "bk": column(L0_gnn_bk), "bv": column(L0_gnn_bv), "bs": column(L0_gnn_bskip),
        "blin": np.ascontiguousarray(L0_gnn_blin), "gamma": np.ascontiguousarray(L0_gnn_gamma),
        "beta": np.ascontiguousarray(L0_gnn_beta),
    }
    nc = bacc.Bacc("TRN2", target_bir_lowering=False, num_devices=1)
    io = {name: nc.dram_tensor(f"in_{name}", a.shape, mybir.dt.from_np(a.dtype), kind="ExternalInput").ap()
          for name, a in arrays.items()}
    io["out"] = nc.dram_tensor("out", (N, D), F32, kind="ExternalOutput").ap()
    build(nc, io)
    result = run_bass_kernel_spmd(nc, [{f"in_{name}": a for name, a in arrays.items()}], core_ids=[0])
    return result.results[0]["out"]
```

```python
from contextlib import ExitStack

import concourse.bass as bass
from concourse import mybir

F32 = mybir.dt.float32
F32R = mybir.dt.float32r
F16 = mybir.dt.float16
I16 = mybir.dt.int16
I32 = mybir.dt.int32
ALU = mybir.AluOpType
ACT = mybir.ActivationFunctionType
AX_X = mybir.AxisListType.X
RMAX = bass.bass_isa.ReduceOp.max

P = 128
N = 1250
D = 512
H = 4
KT = D // P
NT = (N + P - 1) // P
NP = NT * P
LAST = N - (NT - 1) * P
E = 41250
EP = 125
CH = E // EP
J = 10
PARTS = 2
JP = J // PARTS
TB = 3
CB = CH // TB
DIV_SHIFT = 14
DIV = (1 << DIV_SHIFT) // J + 1
assert all((n * DIV) >> DIV_SHIFT == n // J for n in range(CH + J)) and (CH + J) * DIV < 1 << 24
SLOTS = 2
WIN_SLOTS = SLOTS + 2
WIN = 32
NW = NP // WIN
SB = (N + 3) // 4
SBP = SB + SB % 2
SCALE = float(D) ** -0.5
BIG = 1e30
COUNT_SCALE = 4.0
NONE = 2.0 ** -60
NONE_SCALE = 2e28
EPS = 1e-5
CH_N = [(0, 512), (512, 1024), (1024, N)]
X_PARTS = [(0, NT // 2), (NT // 2, NT - 1)]
TG = [(0, 4), (4, 8), (8, NT)]


def rows_of(s):
    return P if s < NT - 1 else LAST


def three(nc, out, l_hi, l_lo, r_hi, r_lo, start, stop):
    nc.tensor.matmul(out, l_hi, r_hi, start=start, stop=False, skip_group_check=True)
    nc.tensor.matmul(out, l_hi, r_lo, start=False, stop=False, skip_group_check=True)
    return nc.tensor.matmul(out, l_lo, r_hi, start=False, stop=stop, skip_group_check=True)


QM, KM, VM, LM, SM = range(5)
NAMES = ("Wq", "Wk", "Wv", "Wl", "Ws")
PAIR = {QM: 0, KM: 1, VM: 2, LM: 3, SM: 2}
WORK = ([("M", 0)], [("M", 1), ("M", 2)], [("M", 3)], [("uw", 0)], [("A", 0)], [("A", 1), ("A", 2)],
        [("A", 3), ("turn", 0)], [("vs", 0)], [("B", 0), ("B", 1)], [("B", 2), ("B", 3)])
RAW = {QM: (2, 1, 0), KM: (1, 2, 0), LM: (1, 2, 1), VM: (0, 2, 0), SM: (0, 2, 1)}
SPLIT = {1: ((VM, 0),), 2: ((LM, 0),), 4: ((KM, 1),), 7: ((SM, 0),), 8: ((QM, 1),)}
FETCH = {0: ((VM, 0), (LM, 0)), 2: ((SM, 0),), 3: ((KM, 1),), 4: ((QM, 1),)}
IN_BANKS = [(kind, m) for work in WORK for kind, m in work if kind != "B"]
WH = NW // H
TILE_WINS = P // WIN
UNROLL = 2
MOST_GROUPS = NW * (CH // J)


def fold_and_count(nc, io, keep, dram, sem):
    with ExitStack() as ctx:
        sb = lambda name, shape, dt: ctx.enter_context(nc.sbuf_tensor(name, shape, dt))
        raw = [sb(f"raw{j}", [P, KT, D], F32) for j in range(3)]
        w_hi = [keep["m_hi"]] + [sb(f"w_hi{m}", [P, KT, D], F32R) for m in range(1, 4)]
        w_lo = [keep["m_lo"]] + [sb(f"w_lo{m}", [P, KT, D], F32R) for m in range(1, 4)]
        o_hi, o_lo = keep["a_hi"], keep["a_lo"]
        xs = keep["h"]
        zero = sb("zero_r", [P, D], F32R)
        ones = sb("ones", [P, P], F32)
        zero16 = sb("zero16", [EP, SB], F16)
        iota_key = sb("iota_key", [EP, P], I16)
        iota_col = sb("iota_col", [EP, SBP], F16)
        win_iota = sb("win_iota", [EP, WIN_SLOTS, P], I16)
        win_key = sb("win_key", [EP, NW + 1], F32)
        key = sb("key", [EP, CH + J - 1, 2], I16)
        col = sb("col", [EP, CH + J - 1, 2], F16)
        bias = sb("bias", [P, 4, H * KT], F32)
        bias_r = sb("bias_r", [P, H * KT, 3, 4], F32R)
        bias_now = sb("bias_now", [P, UNROLL * KT, 3, 4], F32R)
        row_number = sb("row_number", [4, 1], F32)
        pick = sb("pick", [4, 2], F32)
        pick_v, pick_s = sb("pick_v", [4, P], F32), sb("pick_s", [4, P], F32)
        bkq = sb("bkq", [P, H * KT], F32)
        bkq4 = sb("bkq4", [P, H], F32)
        first = sb("first", [P, H], F32)
        tiny = sb("tiny", [P, 1], F32)
        stats = sb("stats1", [P, NT, 6], F32)
        mv = sb("mv1", [P, NT, 2], F32)
        std, rstd, nmr = (sb(f"{x}1", [P, NT], F32) for x in ("std", "rstd", "nmr"))
        ends = sb("ends", [CB, TB, 2], F32)
        win_i = sb("win_i", [CB, NW], F32)
        down, up = sb("down", [CB, TB], F32), sb("up", [CB, TB], F32)
        flag0, flag = sb("flag0", [CB, TB, NW], F32), sb("flag", [CB, TB, NW], F32)
        vals_of, vals, rng = (sb("vals_of", [CB, TB, 2, NW], F32), sb("vals", [CB, 2, NW], F32),
                              sb("rng", [CB, 2, NW], F32))
        first_chunk, chunks = sb("first_chunk", [1, NW], F32), sb("chunks", [1, NW], F32)
        groups_i = sb("groups_i", [1, NW], I32)
        to_last = sb("to_last", [1, NW], F32)
        win_range = sb("win_range", [1, 3, NW], I32)
        with ExitStack() as early:
            tmp = lambda name, dt: early.enter_context(nc.sbuf_tensor(name, [EP, CH], dt))
            src_i, dst_i, dw_i = (tmp(name, I32) for name in ("src_i", "dst_i", "dw_i"))
            srcf, dstf, dwf, blk = (tmp(name, F32) for name in ("srcf", "dstf", "dwf", "blk"))
        hot_key = sb("hot_key", [EP, SLOTS, J, P], F16)
        hot_col = sb("hot_col", [EP, SLOTS, J, SBP], F16)
        flat = sb("logs_and_rows", [P, 8 * SB + 2 * D], F32)
        logs = [flat[:, s * 4 * SB:(s + 1) * 4 * SB] for s in range(2)]
        uw_rows = flat[0:4, 8 * SB:8 * SB + D]
        vs_rows = flat[0:4, 8 * SB + D:8 * SB + 2 * D]

        prod = [ctx.enter_context(nc.psum_tensor(f"prod{j}", [P, D], F32)) for j in range(2)]
        bps = [ctx.enter_context(nc.psum_tensor(f"bps{m}", [P, D], F32)) for m in range(KT)]
        wbank = [ctx.enter_context(nc.psum_tensor(f"wbank{k}", [P, D], F32)) for k in range(2)]
        win = [b[:, 0:SB] for b in wbank]
        dots = wbank[0][:, 448:448 + H]
        gps = [bps[b][0:CB, 0:EP] for b in range(TB)]

        edges_in, bias_in, row_in = sem("edges_in"), sem("bias_in"), sem("row_in")
        x_in = [sem(f"x_in{k}") for k in range(len(X_PARTS) + 1)]
        raw_in = [sem(f"raw_in{j}") for j in range(3)]
        raw_free = [sem(f"raw_free{j}") for j in range(3)]
        pad_done, consts, tiny_done = sem("pad_done"), sem("consts"), sem("tiny_done")
        step_d, dw_done, gt_done, vals_done, rng_done = (sem("dve_step"), sem("dw_done"), sem("gt_done"),
                                                         sem("vals_done"), sem("rng_done"))
        vs_turn, vs_cleared, dve_turn = sem("vs_turn"), sem("vs_cleared"), sem("dve_turn")
        stats_done, var_done, std_done, norm_done = sem("stats_done"), sem("var_done"), sem("std_done"), sem("norm_done")
        h_done, gt_read, dots_taken = sem("h_done"), sem("gt_read"), sem("dots_taken")
        w_hi_done = [sem(f"w_hi_done{m}") for m in range(5)]
        w_lo_done = [sem(f"w_lo_done{m}") for m in range(5)]
        eye_added = sem("eye_added")
        bias_ready, dots_done = sem("bias_ready"), sem("dots_done")
        prod_done, prod_hi, prod_lo, b_done = sem("prod_done"), sem("prod_hi"), sem("prod_lo"), sem("b_done")
        b_part = sem("b_part")
        stored = [sem(f"stored{m}") for m in range(KT)]
        now_ready = sem("now_ready")
        rows_done, m_back = sem("rows_done"), sem("m_back")
        hot_ready = [[sem(f"hot_ready{a}{b}") for b in range(PARTS)] for a in range(SLOTS)]
        hot_free = [[sem(f"hot_free{a}{b}") for b in range(PARTS)] for a in range(SLOTS)]
        win_keys = sem("win_keys")
        win_done = sem("win_done")
        logs_done, masked = sem("logs_done"), sem("masked")
        act_turn, ranges_ready = sem("act_turn"), sem("ranges_ready")
        logs_stored = [sem(f"logs_stored{s}") for s in range(2)]
        block = ctx.enter_context(nc.Block())

        def schedule():
            for hh in range(UNROLL):
                for i in range(WH):
                    yield hh * WH + i, hh, i

        TILES = UNROLL * WH // TILE_WINS
        SLOT_USES = (TILES + 1) // 2, TILES // 2
        MASK_AT = {min(TILE_WINS * (tile + 1) + 1, UNROLL * WH - 1): tile for tile in range(TILES)}


        def slot_uses(rd, tile):
            return SLOT_USES[tile % 2] * rd + tile // 2

        def raw_uses(h, m):
            return RAW[m][1] * h + RAW[m][2]

        def of_head(rd, hh, following):
            h = UNROLL * rd + hh + following
            return h, (h % H if following and hh == UNROLL - 1 else h)

        def quarters(h, kind, m):
            return 8 * h + (0 if kind == "M" else 4) + m

        def in_bank(hh, kind, m):
            n = len(IN_BANKS) * hh + IN_BANKS.index((kind, m))
            return prod[n % 2], n

        PER_ROUND = UNROLL * len(IN_BANKS)

        def done_before(h, kind=None, m=0):
            return len(IN_BANKS) * (h + 1) + (IN_BANKS.index((kind, m)) + 1 if kind else 0)

        @block.sync
        def _(sp):
            sp.dma_start(dst_i[:, :], io["dst"]).then_inc(edges_in, 16)
            sp.dma_start(src_i[:, :], io["src"]).then_inc(edges_in, 16)
            for n, name in enumerate(("bq", "bk", "bv", "bs")):
                sp.dma_start(bias[:, n, :], io[name]).then_inc(bias_in, 16)
            for k, (start, end) in enumerate(X_PARTS):
                rows = io["x"][start * P:end * P, :].rearrange("(t p) d -> p t d", p=P)
                sp.dma_start(xs[:, start:end, :], rows).then_inc(x_in[k], 16)
            sp.wait_ge(pad_done, 1)
            sp.dma_start(xs[0:LAST, NT - 1, :], io["x"][(NT - 1) * P:N, :]).then_inc(x_in[-1], 16)
            for m in (KM, QM):
                sp.dma_start(raw[RAW[m][0]][:, :, :], io[NAMES[m]][0]).then_inc(raw_in[RAW[m][0]], 16)
            sp.dma_start(keep["s_row"][:, :], io["blin"].partition_broadcast(P)).then_inc(row_in, 16)
            for s in range(2):
                sp.sem_inc(logs_stored[s], 16)
            with sp.Fori(0, H // UNROLL) as rd:
                for wi, hh, i in schedule():
                    for m, following in FETCH.get(i, ()):
                        h, source = of_head(rd, hh, following)
                        sp.wait_ge(raw_free[RAW[m][0]], raw_uses(h, m) + 1)
                        sp.dma_start(raw[RAW[m][0]][:, :, :], io[NAMES[m]][bass.ds(source, 1)].rearrange(
                            "a p c n -> (a p) c n")).then_inc(raw_in[RAW[m][0]], 16)
                    if wi in MASK_AT:
                        tile = MASK_AT[wi]
                        t = TILES * rd + tile
                        sp.wait_ge(masked, t + 1)
                        sp.dma_start(dram["L"][bass.ds(t, 1)].rearrange("a p n -> (a p) n"), logs[tile % 2][:, 0:N]
                                     ).then_inc(logs_stored[tile % 2], 16)
            for s in range(2):
                sp.wait_ge(logs_stored[s], 16 * SLOT_USES[s] * (H // UNROLL) + 16)

        @block.gpsimd
        def _(pool):
            for j in range(3):
                pool.sem_inc(raw_free[j], 1)
            nc.gpsimd.memset(xs[:, NT - 1, :], 0.0).then_inc(pad_done, 1)
            nc.gpsimd.memset(keep["ident"][:, :], 1.0).then_inc(pad_done, 1)
            pool.wait_ge(pad_done, 2)
            nc.gpsimd.affine_select(out=keep["ident"][:, :], in_=keep["ident"][:, :], compare_op=ALU.is_equal,
                                    fill=0.0, base=0, pattern=[[-1, P]], channel_multiplier=1).then_inc(consts, 1)
            nc.gpsimd.memset(ones[:, :], 1.0).then_inc(consts, 1)
            nc.gpsimd.memset(zero16[:, :], 0.0).then_inc(consts, 1)
            nc.gpsimd.memset(zero[:, :].bitcast(F32), 0.0).then_inc(consts, 1)

            def iota(out, pattern, base=0, step=0):
                nc.gpsimd.iota(out, pattern=pattern, base=base, channel_multiplier=step,
                               allow_small_or_imprecise_dtypes=True).then_inc(consts, 1)

            nc.gpsimd.memset(bias_r[:, :, :, :].bitcast(F32), 0.0).then_inc(consts, 1)
            iota(row_number[:, :], [[0, 1]], 0, 1)
            iota(win_i[:, :], [[1, NW]])
            iota(up[:, :], [[CB, TB]], 1, 1)
            iota(down[:, :], [[-CB, TB]], CH, -1)
            iota(iota_key[:, :], [[1, P]])
            iota(iota_col[:, :], [[1, SBP]])
            iota(win_key[:, :], [[P, NW + 1]])
            nc.gpsimd.memset(tiny[:, :], NONE).then_inc(tiny_done, 1)
            pool.wait_ge(vals_done, 1)
            nc.gpsimd.partition_all_reduce(rng[:, :, :].rearrange("p a w -> p (a w)"),
                                           vals[:, :, :].rearrange("p a w -> p (a w)"), CB, RMAX).then_inc(rng_done, 1)

            def split_lo(h, m):
                pool.wait_ge(w_hi_done[m], h + 1)
                nc.gpsimd.tensor_tensor(w_lo[PAIR[m]][:, :, :], raw[RAW[m][0]][:, :, :],
                                        w_hi[PAIR[m]][:, :, :].bitcast(F32), ALU.subtract).then_inc(w_lo_done[m], 1)
                pool.wait_ge(w_lo_done[m], h + 1)
                pool.sem_inc(raw_free[RAW[m][0]], 1)

            for m in (KM, QM):
                split_lo(0, m)
            with pool.Fori(0, H // UNROLL) as rd:
                for wi, hh, i in schedule():
                    for m, following in SPLIT.get(i, ()):
                        split_lo(of_head(rd, hh, following)[0], m)
            pool.wait_ge(w_lo_done[QM], H + 1)
            for half, out in enumerate((w_hi[0], w_lo[0])):
                pool.dma_start(out[:, :, :].bitcast(F32), dram["M"][0, half]).then_inc(m_back, 16)
            pool.wait_ge(m_back, 32)

        @block.scalar
        def _(act):
            def split_hi(h, m):
                act.wait_ge(raw_in[RAW[m][0]], 16 * raw_uses(h, m) + 16)
                if m in (QM, KM):
                    act.wait_ge(prod_done, done_before(h - 1, "uw"))
                elif m == SM:
                    act.wait_ge(prod_done, done_before(h, "A", KT - 1))
                else:
                    act.wait_ge(b_part, h + 1)
                if m == LM:
                    act.wait_ge(eye_added, h + 1)
                nc.scalar.copy(w_hi[PAIR[m]][:, :, :], raw[RAW[m][0]][:, :, :]).then_inc(w_hi_done[m], 1)

            def store(taken, lows, m, to):
                act.wait_ge(prod_hi, taken)
                act.wait_ge(prod_lo, lows)
                act.dma_start(to(0)[:, m, :], o_hi[:, m, :].bitcast(F32)).then_inc(stored[m], 16)
                act.dma_start(to(1)[:, m, :], o_lo[:, m, :].bitcast(F32)).then_inc(stored[m], 16)

            def take_product(rd, hh, kind, m):
                bank, n = in_bank(hh, kind, m)
                act.wait_ge(prod_done, done_before(UNROLL * rd) + n + 1)
                act.wait_ge(stored[m], 32 * (2 * (UNROLL * rd + hh) + (kind == "A")) + 32)
                nc.scalar.copy(o_hi[:, m, :], bank[:, :]).then_inc(prod_hi, 1)

            act.sem_inc(logs_done, 2)
            for m in range(KT):
                act.sem_inc(stored[m], 32)
            for m in (KM, QM):
                split_hi(0, m)
            act.wait_ge(var_done, 1)
            nc.scalar.activation(std[:, :], std[:, :], ACT.Sqrt).then_inc(std_done, 1)
            act.wait_ge(norm_done, 1)
            for t in range(NT):
                nc.scalar.activation(xs[:, t, :], xs[:, t, :], ACT.Relu, bias=nmr[:, t:t + 1],
                                     scale=rstd[:, t:t + 1]).then_inc(h_done, 1)
            act.wait_ge(tiny_done, 1)
            act.wait_ge(bias_ready, 1)
            with act.Fori(0, H // UNROLL) as rd:
                pending = []
                act.wait_ge(prod_done, done_before(UNROLL * rd))
                act.sem_inc(act_turn, 1)
                nc.scalar.copy(bias_now[:, :, :, :], bias_r[:, bass.ds(UNROLL * KT * rd, UNROLL * KT)]).then_inc(now_ready, 1)
                for wi, hh, i in schedule():
                    h = UNROLL * rd + hh
                    for m, following in SPLIT.get(i, ()):
                        split_hi(of_head(rd, hh, following)[0], m)
                    k, tile = wi % TILE_WINS, wi // TILE_WINS
                    w = UNROLL * WH * rd + wi
                    act.wait_ge(win_done, w + 1)
                    if k == 0:
                        act.wait_ge(logs_stored[tile % 2], 16 * slot_uses(rd, tile) + 16)
                    for a in range(TILE_WINS):
                        last = nc.scalar.activation(logs[tile % 2][k * WIN:(k + 1) * WIN, a * SB:(a + 1) * SB],
                                                    win[wi % 2][a * WIN:(a + 1) * WIN, :], ACT.Ln,
                                                    bias=tiny[a * WIN:(a + 1) * WIN, :], scale=COUNT_SCALE)
                    last.then_inc(logs_done, 1)
                    for kind, m, before in pending:
                        store(quarters(UNROLL * rd + before, kind, m) + 1,
                              PER_ROUND * rd + in_bank(before, kind, m)[1] + 3,
                              m, lambda half, kind=kind, h=UNROLL * rd + before: dram[kind][
                            bass.ds(h, 1), half].rearrange("a p c n -> (a p) c n"))
                    pending = [(kind, m, hh) for kind, m in WORK[i] if kind in "MA"]
                    for kind, m in WORK[i]:
                        if kind in "MA":
                            take_product(rd, hh, kind, m)
            act.wait_ge(b_done, 1)
            act.wait_ge(h_done, NT)
            for m in range(KT):
                act.wait_ge(stored[m], 16 * 4 * H + 32)
                nc.scalar.copy(o_hi[:, m, :], bps[m][:, :]).then_inc(prod_hi, 1)
            act.wait_ge(rows_done, 1)
            nc.scalar.copy(keep["v_row"][:, :], prod[0][:, :])

        @block.vector
        def _(dve):
            count = [0]
            arrivals = {start: k for k, (start, end) in enumerate(X_PARTS + [(NT - 1, NT)])}
            rows_left = list(range(NT))

            def sums_of_x(tiles):
                for _ in range(tiles):
                    t = rows_left.pop(0)
                    if t in arrivals:
                        dve.wait_ge(x_in[arrivals[t]], 16)
                    nc.vector.bn_stats(stats[:, t, :], xs[:, t, :]).then_inc(stats_done, 1)

            def step(ins, tiles=0):
                count[0] += 1
                ins.then_inc(step_d, 1)
                sums_of_x(tiles)
                dve.wait_ge(step_d, count[0])

            dve.sem_inc(prod_lo, 2)
            dve.wait_ge(edges_in, 32)
            step(nc.vector.tensor_scalar(dw_i[:, :], dst_i[:, :], 5, None, ALU.arith_shift_right))
            nc.vector.tensor_copy(dwf[:, :], dw_i[:, :]).then_inc(dw_done, 1)
            nc.vector.tensor_copy(dstf[:, :], dst_i[:, :])
            step(nc.vector.tensor_copy(srcf[:, :], src_i[:, :]))
            step(nc.vector.tensor_scalar(blk[:, :], srcf[:, :], float(SB), None, ALU.is_ge))
            for a in (2, 3):
                step(nc.vector.scalar_tensor_tensor(out=blk[:, :], in0=srcf[:, :], scalar=float(a * SB),
                                                    in1=blk[:, :], op0=ALU.is_ge, op1=ALU.add))
            dve.wait_ge(dw_done, 1)
            step(nc.vector.scalar_tensor_tensor(out=dstf[:, :], in0=dwf[:, :], scalar=float(P - WIN),
                                                in1=dstf[:, :], op0=ALU.mult, op1=ALU.add))
            dve.wait_ge(gt_done, 1)
            for b in range(TB):
                nc.vector.tensor_reduce(ends[:, b, 0:1], gps[b], AX_X, ALU.min)
                last = nc.vector.tensor_reduce(ends[:, b, 1:2], gps[b], AX_X, ALU.max)
            step(last, 1)
            dve.sem_inc(gt_read, 1)
            dve.wait_ge(consts, 12)
            for b in range(TB):
                last = nc.vector.tensor_scalar(flag0[:, b, :], win_i[:, :], ends[:, b, 0:1], None, ALU.is_ge)
            step(last, 1)
            for b in range(TB):
                last = nc.vector.scalar_tensor_tensor(out=flag[:, b, :], in0=win_i[:, :], scalar=ends[:, b, 1:2],
                                                      in1=flag0[:, b, :], op0=ALU.is_le, op1=ALU.mult)
            step(last, 1)
            for b in range(TB):
                nc.vector.tensor_scalar(vals_of[:, b, 0, :], flag[:, b, :], down[:, b:b + 1], None, ALU.mult)
                last = nc.vector.tensor_scalar(vals_of[:, b, 1, :], flag[:, b, :], up[:, b:b + 1], None, ALU.mult)
            step(last, 1)
            step(nc.vector.tensor_tensor(vals[:, :, :], vals_of[:, 0, :, :], vals_of[:, 1, :, :], ALU.max), 1)
            nc.vector.tensor_tensor(vals[:, :, :], vals[:, :, :], vals_of[:, 2, :, :], ALU.max).then_inc(vals_done, 1)
            for k in range(2):
                nc.vector.scalar_tensor_tensor(out=col[:, 0:CH, k], in0=blk[:, :], scalar=-float(SB),
                                               in1=srcf[:, :], op0=ALU.mult, op1=ALU.add)
                nc.vector.scalar_tensor_tensor(out=key[:, 0:CH, k], in0=blk[:, :], scalar=float(WIN),
                                               in1=dstf[:, :], op0=ALU.mult, op1=ALU.add)
            nc.vector.memset(key[:, CH:, :], -1)
            step(nc.vector.memset(col[:, CH:, :], 0.0))

            dve.wait_ge(bias_in, 64)
            for n, (group, at) in enumerate(((0, 0), (1, 2), (2, 0), (2, 2))):
                hi, lo = bias_r[:, :, group, at], bias_r[:, :, group, at + 1]
                step(nc.vector.tensor_copy(hi, bias[:, n, :]))
                nc.vector.tensor_tensor(lo, bias[:, n, :], hi.bitcast(F32), ALU.subtract)
            nc.vector.tensor_scalar(pick[:, 0:1], row_number[:, :], 2.0, None, ALU.is_lt)
            step(nc.vector.tensor_scalar(pick[:, 1:2], row_number[:, :], 2.0, None, ALU.is_ge))
            for n, out in enumerate((pick_v, pick_s)):
                nc.vector.tensor_scalar(out[:, :], ones[0:4, :], pick[:, n:n + 1], None, ALU.mult)
            step(nc.vector.tensor_tensor(bkq[:, :], bias[:, 0, :], bias[:, 1, :], ALU.mult))
            nc.vector.tensor_reduce(bkq4[:, :], bkq[:, :].rearrange("p (h c) -> p h c", h=H), AX_X,
                                    ALU.add).then_inc(bias_ready, 1)
            step(nc.vector.memset(first[:, :], 0.0))
            step(nc.vector.memset(first[:, 0:1], 1.0))

            sums_of_x(len(rows_left))
            dve.wait_ge(stats_done, NT)
            for t in range(NT):
                last = nc.vector.bn_aggr(mv[:, t, :], stats[:, t, :])
            step(last)
            nc.vector.tensor_scalar(std[:, :], mv[:, :, 1], EPS, None, ALU.add).then_inc(var_done, 1)
            dve.wait_ge(std_done, 1)
            step(nc.vector.reciprocal(rstd[:, :], std[:, :]))
            nc.vector.scalar_tensor_tensor(out=nmr[:, :], in0=mv[:, :, 0], scalar=-1.0, in1=rstd[:, :],
                                           op0=ALU.mult, op1=ALU.mult).then_inc(norm_done, 1)

            dve.wait_ge(rng_done, 1)
            step(nc.vector.tensor_scalar(first_chunk[:, :], rng[0:1, 0, :], -1.0, float(CH), ALU.mult, ALU.add))
            step(nc.vector.tensor_scalar(first_chunk[:, :], first_chunk[:, :], float(CH - 1), None, ALU.min))
            step(nc.vector.tensor_tensor(chunks[:, :], rng[0:1, 1, :], first_chunk[:, :], ALU.subtract))
            step(nc.vector.tensor_scalar(chunks[:, :], chunks[:, :], 1.0, float(J - 1), ALU.max, ALU.add))
            step(nc.vector.tensor_scalar(groups_i[:, :], chunks[:, :], float(DIV), None, ALU.mult))
            step(nc.vector.tensor_scalar(win_range[:, 2, :], groups_i[:, :], DIV_SHIFT, None, ALU.arith_shift_right))
            step(nc.vector.tensor_scalar(to_last[:, :], win_range[:, 2, :], float(J), float(1 - J), ALU.mult, ALU.add))
            nc.vector.tensor_tensor(win_range[:, 1, :], to_last[:, :], first_chunk[:, :], ALU.add)
            nc.vector.tensor_copy(win_range[:, 0, :], first_chunk[:, :]).then_inc(ranges_ready, 1)
            dve.wait_ge(dots_done, 1)
            nc.vector.tensor_copy(keep["bqbk"][:, :], dots).then_inc(dots_taken, 1)

            dve.wait_ge(ranges_ready, 1)
            turns = [dve.alloc_register(f"dve_turn{k}") for k in range(SLOTS)]
            for turn in turns:
                dve.reg_mov(turn, 1)

            def keys_of(w, slot):
                nc.vector.tensor_scalar(win_iota[:, slot, :], iota_key[:, :], win_key[:, bass.ds(w, 1)], None, ALU.add
                                        ).then_inc(win_keys, 1)

            keys_of(0, 0)
            nc.vector.memset(vs_rows, 0.0).then_inc(vs_cleared, 1)
            with dve.Fori(0, H // UNROLL) as rd:
                pending = []
                for wi, hh, i in schedule():
                    h = UNROLL * rd + hh
                    w = UNROLL * WH * rd + wi
                    if i == 2:
                        dve.wait_ge(raw_in[RAW[LM][0]], 16 * raw_uses(h, LM) + 16)
                        for c in range(KT):
                            d = raw[RAW[LM][0]][:, c, c * P:(c + 1) * P]
                            last = nc.vector.scalar_tensor_tensor(out=d, in0=keep["ident"][:, :],
                                                                  scalar=first[:, bass.ds(h, 1)], in1=d,
                                                                  op0=ALU.mult, op1=ALU.add)
                        last.then_inc(eye_added, 1)
                    lo = dve.value_load(win_range[0:1, 0, bass.ds(w, 1)], min_val=0, max_val=CH - 1)
                    end = dve.value_load(win_range[0:1, 1, bass.ds(w, 1)], min_val=1, max_val=CH)
                    dve.wait_ge(win_keys, w + 1)
                    dve.sem_inc(dve_turn, 1)
                    slot, turn = wi % SLOTS, turns[wi % SLOTS]
                    with dve.Fori(lo, end, J) as chunk:
                        n = dve.snap(turn, min_val=1, max_val=MOST_GROUPS)
                        keys = win_iota[:, wi % WIN_SLOTS, :].rearrange("p (o c b) -> p o c b", o=1, b=2)
                        cols = iota_col[:, :].rearrange("p (o c b) -> p o c b", o=1, b=2)
                        for part in range(PARTS):
                            mine = slice(part * JP, part * JP + JP)
                            dve.wait_ge(hot_free[slot][part], n)
                            nc.vector.tensor_tensor(
                                hot_key[:, slot, mine].rearrange("p j (c b) -> p j c b", b=2),
                                keys.broadcast_to([EP, JP, P // 2, 2]),
                                key[:, bass.ds(chunk + part * JP, JP), :].rearrange("p j (o b) -> p j o b", o=1
                                                                                    ).broadcast_to([EP, JP, P // 2, 2]),
                                ALU.is_equal)
                            nc.vector.tensor_tensor(
                                hot_col[:, slot, mine].rearrange("p j (c b) -> p j c b", b=2),
                                cols.broadcast_to([EP, JP, SBP // 2, 2]),
                                col[:, bass.ds(chunk + part * JP, JP), :].rearrange("p j (o b) -> p j o b", o=1
                                                                                    ).broadcast_to([EP, JP, SBP // 2, 2]),
                                ALU.is_equal).then_inc(hot_ready[slot][part], 1)
                        dve.reg_add(turn, turn, 1)
                    keys_of(w + 1, (wi + 1) % WIN_SLOTS)
                    if wi in MASK_AT:
                        tile = MASK_AT[wi]
                        dve.wait_ge(logs_done, TILE_WINS * (TILES * rd + tile + 1) + 2)
                        dve.sem_inc(dve_turn, 1)
                        now = logs[tile % 2][:, 0:N]
                        nc.vector.scalar_tensor_tensor(out=now, in0=now, scalar=NONE_SCALE, in1=now, op0=ALU.mult,
                                                       op1=ALU.min).then_inc(masked, 1)
                    for kind, m, before in pending:
                        bank, n = in_bank(before, kind, m)
                        if kind in "MA":
                            dve.wait_ge(prod_hi, quarters(UNROLL * rd + before, kind, m) + 1)
                            nc.vector.tensor_tensor(o_lo[:, m, :], bank[:, :], o_hi[:, m, :].bitcast(F32),
                                                    ALU.subtract).then_inc(prod_lo, 1)
                            continue
                        dve.wait_ge(prod_done, done_before(UNROLL * rd) + n + 1)
                        if kind == "uw":
                            nc.vector.tensor_copy(uw_rows, bank[0:4, :]).then_inc(prod_lo, 1)
                        elif kind == "vs":
                            dve.wait_ge(vs_cleared, 1)
                            dve.sem_inc(vs_turn, 1)
                            nc.vector.tensor_tensor(vs_rows, bank[0:4, :], vs_rows, ALU.add).then_inc(prod_lo, 1)
                        else:
                            dve.sem_inc(vs_turn, 1)
                            nc.vector.tensor_copy(
                                keep["uw"][:, :, bass.ds(UNROLL * rd + before, 1)].rearrange(
                                    "p (k m) a -> p k (m a)", k=2),
                                bank[:, 0:2 * KT].rearrange("p (m k) -> p k m", k=2)).then_inc(prod_lo, 1)
                    pending = [(kind, m, hh) for kind, m in WORK[i] if kind != "B"]
            dve.wait_ge(b_done, 1)
            for m in range(KT):
                dve.wait_ge(prod_hi, 8 * H + m + 1)
                nc.vector.tensor_tensor(o_lo[:, m, :], bps[m][:, :], o_hi[:, m, :].bitcast(F32),
                                        ALU.subtract).then_inc(prod_lo, 1)
            dve.wait_ge(rows_done, 1)
            dve.wait_ge(row_in, 16)
            nc.vector.tensor_tensor(keep["s_row"][:, :], prod[1][:, :], keep["s_row"][:, :], ALU.add)

        @block.tensor
        def _(pe):
            def product(out, a, b, m, start, stop):
                a, b = PAIR[a], PAIR[b]
                for c in range(KT):
                    last = three(nc, out, w_hi[a][:, c, m * P:(m + 1) * P], w_lo[a][:, c, m * P:(m + 1) * P],
                                 w_hi[b][:, c, :], w_lo[b][:, c, :], start and c == 0, stop and c == KT - 1)
                return last

            def bias_rows(out, hh, group, matrix, start, stop):
                for c in range(KT):
                    for half, w in enumerate((w_hi, w_lo)):
                        last = nc.tensor.matmul(out[0:4, :], bias_now[:, hh * KT + c, group, :], w[PAIR[matrix]][:, c, :],
                                                start=start and c == 0 and half == 0,
                                                stop=stop and c == KT - 1 and half == 1, skip_group_check=True)
                return last

            def work(rd, hh, kind, m):
                h = UNROLL * rd + hh
                if kind == "B":
                    if m == 0:
                        pe.wait_ge(w_lo_done[SM], h + 1)
                    last = product(bps[m][:, :], SM, LM, m, False, False)
                    if m == KT - 1:
                        last.then_inc(b_part, 1)
                    return
                out, n = in_bank(hh, kind, m)
                pe.wait_ge(prod_lo, PER_ROUND * rd + n + 1)
                if kind in "MA":
                    a, b = (QM, KM) if kind == "M" else (VM, LM)
                    if m == 0:
                        pe.wait_ge(w_lo_done[a], h + 1)
                        pe.wait_ge(w_lo_done[b], h + 1)
                    last = product(out[:, :], a, b, m, True, True)
                elif kind == "uw":
                    pe.wait_ge(now_ready, rd + 1)
                    bias_rows(out, hh, 0, KM, True, False)
                    last = bias_rows(out, hh, 1, QM, False, True)
                elif kind == "vs":
                    last = bias_rows(out, hh, 2, LM, True, True)
                else:
                    pe.wait_ge(prod_lo, PER_ROUND * rd + in_bank(hh, "uw", 0)[1] + 3)
                    for m in range(KT):
                        last = nc.tensor.matmul(out[:, 2 * m:2 * m + 2], uw_rows[:, m * P:(m + 1) * P], pick[:, :],
                                                start=True, stop=True)
                last.then_inc(prod_done, 1)

            for slot in range(SLOTS):
                for part in range(PARTS):
                    pe.sem_inc(hot_free[slot][part], 1)
            pe.sem_inc(prod_done, len(IN_BANKS))
            pe.sem_inc(b_part, 1)
            pe.wait_ge(consts, 4)
            pe.wait_ge(dw_done, 1)
            for b in range(TB):
                last = nc.tensor.transpose(gps[b], dwf[:, b * CB:(b + 1) * CB], keep["ident"][0:EP, 0:EP])
            last.then_inc(gt_done, 1)
            pe.wait_ge(bias_ready, 1)
            nc.tensor.matmul(dots, ones[:, :], bkq4[:, :], start=True, stop=True).then_inc(dots_done, 1)
            pe.wait_ge(gt_read, 1)
            pe.wait_ge(dots_taken, 1)
            pe.wait_ge(ranges_ready, 1)
            for m in range(KT):
                nc.tensor.matmul(bps[m][:, :], zero[:, 0:P], zero[:, :], start=True, stop=False, skip_group_check=True)
            turns = [pe.alloc_register(f"pe_turn{k}") for k in range(SLOTS)]
            for turn in turns:
                pe.reg_mov(turn, 1)
            with pe.Fori(0, H // UNROLL) as rd:
                for wi, hh, i in schedule():
                    h = UNROLL * rd + hh
                    w = UNROLL * WH * rd + wi
                    groups = pe.value_load(win_range[0:1, 2, bass.ds(w, 1)], min_val=1, max_val=CH // J)
                    pe.wait_ge(logs_done, w + 1)
                    nc.tensor.matmul(win[wi % 2], zero16[:, 0:P], zero16[:, 0:SB], start=True, stop=False,
                                     skip_group_check=True)
                    slot, turn = wi % SLOTS, turns[wi % SLOTS]
                    with pe.Fori(0, groups):
                        n = pe.snap(turn, min_val=1, max_val=MOST_GROUPS)
                        for part in range(PARTS):
                            pe.wait_ge(hot_ready[slot][part], n)
                            for j in range(part * JP, part * JP + JP):
                                last = nc.tensor.matmul(win[wi % 2], hot_key[:, slot, j, :], hot_col[:, slot, j, 0:SB],
                                                        start=False, stop=False, skip_group_check=True)
                            last.then_inc(hot_free[slot][part], 1)
                        pe.reg_add(turn, turn, 1)
                    nc.tensor.matmul(win[wi % 2][:, 0:2], zero16[:, 0:P], zero16[:, 0:2], start=False, stop=True,
                                     skip_group_check=True).then_inc(win_done, 1)
                    for kind, m in WORK[i]:
                        work(rd, hh, kind, m)
            for m in range(KT):
                last = nc.tensor.matmul(bps[m][:, 0:2], zero[:, 0:P], zero[:, 0:2], start=False, stop=True,
                                        skip_group_check=True)
            last.then_inc(b_done, 1)
            pe.wait_ge(prod_lo, PER_ROUND * (H // UNROLL) + 2)
            nc.tensor.matmul(prod[0][:, :], pick_v[:, :], vs_rows, start=True, stop=True)
            nc.tensor.matmul(prod[1][:, :], pick_s[:, :], vs_rows, start=True, stop=True).then_inc(rows_done, 1)


def attend(nc, io, keep, dram, sem):
    with ExitStack() as ctx:
        sb = lambda name, shape, dt: ctx.enter_context(nc.sbuf_tensor(name, shape, dt))
        m_r = [keep["m_hi"], keep["m_lo"]]
        a_r = [keep["a_hi"], keep["a_lo"]]
        g_r = [sb(f"g_{x}", [P, NT, D], F32R) for x in ("hi", "lo")]
        qt_r = [sb(f"qt_{x}", [P, KT, P], F32R) for x in ("hi", "lo")]
        pt_r = [sb(f"pt_{x}", [P, NT, P], F32R) for x in ("hi", "lo")]
        q = sb("q", [P, KT, NP], F32)
        y = keep["h"]
        probs = sb("probs", [P, N], F32)
        logs = sb("logs_in", [P, N], F32)
        w_r = sb("w_r", [P, KT, 2, H], F32R)
        r = sb("r", [P, H * NT], F32)
        r2 = sb("r2", [P, NT, 2 * H], F32)
        r3 = sb("r3", [P, NT, H], F32)
        has = sb("has", [P, NT], F32)
        u = sb("u", [P, KT], F32)
        mx, amax, shift, den, total, share = (sb(x, [P, 1], F32) for x in ("mx", "amax", "shift", "den", "total", "share"))
        gamma = sb("gamma", [P, D], F32)
        beta = sb("beta", [P, D], F32)
        stats = sb("stats2", [P, NT, 6], F32)
        mv = sb("mv2", [P, NT, 2], F32)
        std = sb("std2", [P, NT], F32)
        rstd = sb("rstd2", [P, NT], F32)
        nmr = sb("nmr2", [P, NT], F32)
        x = q[:, :, :].rearrange("p c n -> p (c n)").rearrange("p (t d) -> p t d", t=NT)
        h_r = [sb(f"hT_{x}", [P, KT, NP], F32R) for x in ("hi", "lo")]

        sps = ctx.enter_context(nc.psum_tensor("sps", [P, 3 * 512], F32))
        tps = [ctx.enter_context(nc.psum_tensor(f"tps{g}", [P, 4, P], F32)) for g in range(len(TG))]
        wps = [ctx.enter_context(nc.psum_tensor(f"wps{b}", [P, 512], F32)) for b in range(2)]

        m_in, a_in, logs_in, row_in, x_in = sem("m_in"), sem("a_in"), sem("logs_arrived"), sem("row_in2"), sem("x_in2")
        m_used, a_used, logs_used = sem("m_used"), sem("a_used"), sem("logs_used")
        w_done = [sem(f"w_done{b}") for b in range(2)]
        w_free = [sem(f"w_free{b}") for b in range(2)]
        qt_hi, qt_lo, g_hi, g_lo = sem("qt_hi_done"), sem("qt_lo_done"), sem("g_hi_done"), sem("g_lo_done")
        s_done, shift_done, exp_done = sem("s_done"), sem("shift_done"), sem("exp_done")
        t_done, pt_hi, pt_lo = sem("t_done"), sem("pt_hi_done"), sem("pt_lo_done")
        w_r_done, r_done, r_out, r_turned, r_ready = (sem("w_r_done"), sem("r_done"), sem("r_out"), sem("r_turned"),
                                                      sem("r_ready"))
        chain, mx_done, amax_done, total_done, share_done = (sem("chain"), sem("mx_done"), sem("amax_done"),
                                                           sem("total_done"), sem("share_done"))
        m_ready, q_padded = sem("m_ready"), sem("q_padded")
        ht_done, ht_hi, ht_lo = sem("ht_done"), sem("ht_hi_done"), sem("ht_lo_done")
        u_done, row_turn, r2_cleared = sem("u_done"), sem("row_turn"), sem("r2_cleared")
        st_done, yb_done = sem("st_done"), sem("yb_done")
        var_done, std_done, norm_ready = sem("var_done"), sem("std_done2"), sem("norm_ready")
        z_done, zg_done, xb_done, out_early, out_late, out_stored = (
            sem("z_done"), sem("zg_done"), sem("xb_done"), sem("out_early"), sem("out_late"), sem("out_stored"))
        block = ctx.enter_context(nc.Block())
        W0, W1, START = 11 + NT, 11, NT // 2
        hps = tps[1:]
        EARLY = NT - 3
        BATCHES = [(0, EARLY), (EARLY, NT - 1), (NT - 1, NT)]

        def use(h, i):
            return START + (W0, W1)[i % 2] * h + i // 2

        def use_pv(h, t):
            return START + W0 * h + 11 + t

        @block.sync
        def _(sp):
            sp.dma_start(gamma[:, :], io["gamma"].partition_broadcast(P)).then_inc(row_in, 16)
            sp.dma_start(beta[:, :], io["beta"].partition_broadcast(P)).then_inc(row_in, 16)
            with sp.Fori(0, H) as h:
                with sp.Fori(0, NT) as t:
                    sp.wait_ge(logs_used, NT * h + t + 1)
                    sp.dma_start(logs[:, :], dram["L"][bass.ds(t, 1)].rearrange("a p n -> (a p) n")
                                 ).then_inc(logs_in, 16)
            sp.wait_ge(qt_lo, H * NT)
            for start, end in ((0, NT // 2), (NT // 2, NT - 1)):
                sp.dma_start(x[:, start:end, :], io["x"][start * P:end * P, :].rearrange("(t p) d -> p t d", p=P)
                             ).then_inc(x_in, 16)
            sp.dma_start(x[0:LAST, NT - 1, :], io["x"][(NT - 1) * P:N, :]).then_inc(x_in, 16)
            with sp.Fori(0, EARLY) as t:
                sp.wait_ge(out_early, t + 1)
                sp.dma_start(io["out"][bass.ds(t * P, P), :], y[:, bass.ds(t, 1), :].rearrange("p a d -> p (a d)")
                             ).then_inc(out_stored, 16)
            for t in range(EARLY, NT):
                sp.wait_ge(out_late, t - EARLY + 1)
                p = rows_of(t)
                sp.dma_start(io["out"][t * P:t * P + p, :], y[0:p, t, :]).then_inc(out_stored, 16)
            sp.wait_ge(out_stored, 16 * NT)

        @block.gpsimd
        def _(pool):
            nc.gpsimd.memset(q[:, :, N:NP], 0.0).then_inc(q_padded, 1)
            for h in range(H):
                if h > 0:
                    pool.wait_ge(m_used, h)
                    for half in range(2):
                        pool.dma_start(m_r[half][:, :, :].bitcast(F32), dram["M"][h, half]).then_inc(m_in, 16)
                    pool.wait_ge(m_in, 32 * h)
                    pool.sem_inc(m_ready, 1)
                pool.wait_ge(a_used, h + 1)
                for half in range(2):
                    pool.dma_start(a_r[half][:, :, :].bitcast(F32), dram["A"][h, half]).then_inc(a_in, 16)
            pool.wait_ge(x_in, 48)
            pool.wait_ge(row_in, 32)
            for t in range(NT):
                p = rows_of(t)
                nc.gpsimd.tensor_tensor(x[0:p, t, :], x[0:p, t, :], beta[0:p, :], ALU.add).then_inc(xb_done, 1)
            for t in range(EARLY):
                pool.wait_ge(xb_done, t + 1)
                pool.wait_ge(zg_done, t + 1)
                nc.gpsimd.tensor_tensor(y[:, t, :], y[:, t, :], x[:, t, :], ALU.add).then_inc(out_early, 1)

        @block.tensor
        def _(pe):
            def scores(c, n):
                a, b = CH_N[c]
                for k in range(KT):
                    last = three(nc, sps[:, a:b], qt_r[0][:, k, :], qt_r[1][:, k, :], h_r[0][:, k, a:b],
                                 h_r[1][:, k, a:b], k == 0, k == KT - 1)
                if c == len(CH_N) - 1:
                    last.then_inc(s_done, 1)

            def transposes(g, n):
                pe.wait_ge(pt_lo, 3 * n + g + 1)
                a, b = TG[g]
                for s in range(a, b):
                    last = nc.tensor.transpose(tps[g][0:rows_of(s), s - a, :], probs[:, s * P:s * P + rows_of(s)],
                                               keep["ident"][:, :])
                last.then_inc(t_done, 1)

            def apply(h, t, n):
                pe.wait_ge(w_free[0], use_pv(h, t) + 1)
                pe.wait_ge(g_lo, NT * h + NT)
                for g, (a, b) in enumerate(TG):
                    pe.wait_ge(pt_lo, 3 * n + g + 4)
                    for s in range(a, b):
                        p = rows_of(s)
                        last = three(nc, wps[0][:, :], pt_r[0][0:p, s, :], pt_r[1][0:p, s, :], g_r[0][0:p, s, :],
                                     g_r[1][0:p, s, :], s == 0, s == NT - 1)
                last.then_inc(w_done[0], 1)

            def rows_times(s, i, before):
                b = i % 2
                pe.wait_ge(w_free[b], before + 1)
                for k in range(KT):
                    last = three(nc, wps[b][:, :], h_r[0][:, k, s * P:(s + 1) * P], h_r[1][:, k, s * P:(s + 1) * P],
                                 a_r[0][:, k, :], a_r[1][:, k, :], k == 0, k == KT - 1)
                last.then_inc(w_done[b], 1)

            pe.sem_inc(s_done, 1)
            pe.sem_inc(m_ready, 1)
            def turn_h(t):
                pe.wait_ge(ht_lo, t + 1)
                for c in range(KT):
                    last = nc.tensor.transpose(hps[t % 2][:, c, :], y[:, t, c * P:(c + 1) * P], keep["ident"][:, :])
                last.then_inc(ht_done, 1)

            pe.sem_inc(ht_lo, 2)
            turn_h(0)
            turn_h(1)
            for s in range(NT):
                if s == NT - 1:
                    pe.wait_ge(ht_lo, NT + 2)
                    pe.wait_ge(w_r_done, 1)
                    for a, b in CH_N:
                        for k in range(KT):
                            for half in range(2):
                                last = nc.tensor.matmul(sps[0:2 * H, a:b], w_r[:, k, :, :].rearrange("p a h -> p (a h)"),
                                                        h_r[half][:, k, a:b], start=(k == 0 and half == 0),
                                                        stop=(k == KT - 1 and half == 1))
                    last.then_inc(r_done, 1)
                pe.wait_ge(ht_lo, s + 3)
                rows_times(s, s, s // 2)
                if s + 2 < NT:
                    turn_h(s + 2)
            pe.wait_ge(r_out, 1)
            for t in range(NT):
                last = nc.tensor.transpose(tps[0][0:rows_of(t), 0, t * 2 * H:(t + 1) * 2 * H],
                                           probs[0:2 * H, t * P:t * P + rows_of(t)], keep["ident"][0:2 * H, 0:2 * H])
            last.then_inc(r_turned, 1)
            pe.wait_ge(w_done[1], START)
            pe.sem_inc(a_used, 1)
            with pe.Fori(0, H) as h:
                pe.wait_ge(m_ready, h + 1)
                for m in range(KT):
                    for c, (a, b) in enumerate(CH_N):
                        i = 3 * m + c
                        pe.wait_ge(w_free[i % 2], use(h, i) + 1)
                        for k in range(KT):
                            last = three(nc, wps[i % 2][:, 0:b - a], m_r[0][:, k, m * P:(m + 1) * P],
                                         m_r[1][:, k, m * P:(m + 1) * P], h_r[0][:, k, a:b], h_r[1][:, k, a:b],
                                         k == 0, k == KT - 1)
                        last.then_inc(w_done[i % 2], 1)
                pe.wait_ge(w_done[1], use(h, 11) + 1)
                pe.sem_inc(m_used, 1)
                pe.wait_ge(a_in, 32 * h + 32)
                for s in range(NT // 2):
                    rows_times(s, 12 + s, use(h, 12 + s))
                pe.wait_ge(r_ready, 1)
                pe.wait_ge(qt_lo, NT * h + 1)
                for c in range(len(CH_N)):
                    scores(c, NT * h)
                for s in range(NT // 2, NT):
                    rows_times(s, 12 + s, use(h, 12 + s))
                pe.wait_ge(w_done[1], use(h, 21) + 1)
                pe.sem_inc(a_used, 1)
                with pe.Fori(0, NT - 1) as t:
                    n = NT * h + t
                    pe.wait_ge(exp_done, n + 1)
                    for g in range(len(TG)):
                        transposes(g, n)
                        if g == 0:
                            pe.wait_ge(qt_lo, n + 2)
                        scores(g, n + 1)
                    apply(h, t, n)
                n = NT * h + NT - 1
                pe.wait_ge(exp_done, n + 1)
                for g in range(len(TG)):
                    transposes(g, n)
                apply(h, NT - 1, n)

        @block.scalar
        def _(act):
            def q_hi(h, t, n):
                act.wait_ge(s_done, n + 1)
                nc.scalar.copy(qt_r[0][:, :, :], q[:, :, bass.ds(t * P, P)]).then_inc(qt_hi, 1)

            def softmax(n):
                act.wait_ge(shift_done, n + 1)
                nc.scalar.activation(probs[:, :], sps[:, 0:N], ACT.Exp, bias=shift[:, :],
                                     accum_out=den[:, :]).then_inc(exp_done, 1)

            def take_g(h, s):
                i = 12 + s
                act.wait_ge(w_done[i % 2], use(h, i) + 1)
                nc.scalar.copy(g_r[0][:, s, :], wps[i % 2][:, :]).then_inc(g_hi, 1)

            def take_pt(n):
                for g, (a, b) in enumerate(TG):
                    act.wait_ge(t_done, 3 * n + g + 1)
                    whole = [s for s in range(a, b) if rows_of(s) == P]
                    z = a + len(whole)
                    last = nc.scalar.copy(pt_r[0][:, a:z, :], tps[g][:, 0:z - a, :])
                    if z < b:
                        last = nc.scalar.copy(pt_r[0][0:LAST, z, :], tps[g][0:LAST, z - a, :])
                    last.then_inc(pt_hi, 1)

            act.sem_inc(w_free[0], 1)
            act.sem_inc(w_free[1], 1)
            for t in range(NT):
                act.wait_ge(ht_done, t + 1)
                nc.scalar.copy(h_r[0][:, :, t * P:(t + 1) * P], hps[t % 2][:, :, :]).then_inc(ht_hi, 1)
            act.wait_ge(q_padded, 1)
            def start_head(h):
                nc.scalar.mul(u[:, :], keep["uw"][:, 0:KT, bass.ds(h, 1)].rearrange("p c a -> p (c a)"), SCALE
                              ).then_inc(u_done, 1)
                act.wait_ge(u_done, h + 1)
                for m in range(KT):
                    for c, (a, b) in enumerate(CH_N):
                        i = 3 * m + c
                        act.wait_ge(w_done[i % 2], use(h, i) + 1)
                        nc.scalar.activation(q[:, m, a:b], wps[i % 2][:, 0:b - a], ACT.Identity,
                                             bias=u[:, m:m + 1], scale=SCALE).then_inc(w_free[i % 2], 1)
                act.wait_ge(w_free[0], use(h, 10) + 2)
                act.wait_ge(w_free[1], use(h, 11) + 2)
                q_hi(h, 0, NT * h)
                for s in range(NT // 2):
                    take_g(h, s)
                q_hi(h, 1, NT * h + 1)
                take_g(h, NT // 2)
                softmax(NT * h)
                for s in range(NT // 2 + 1, NT):
                    take_g(h, s)

            def step(h, t):
                n = NT * h + t
                take_pt(n)
                q_hi(h, t + 2, n + 2)
                softmax(n + 1)

            def batch_std(b):
                start, end = BATCHES[b]
                act.wait_ge(var_done, b + 1)
                nc.scalar.activation(std[:, start:end], std[:, start:end], ACT.Sqrt).then_inc(std_done, 1)
                act.wait_ge(norm_ready, b + 1)

            def z(start, end):
                for t in range(start, end):
                    nc.scalar.activation(y[:, t, :], y[:, t, :], ACT.Identity, bias=nmr[:, t:t + 1],
                                         scale=rstd[:, t:t + 1]).then_inc(z_done, 1)

            with act.Fori(0, H - 1) as h:
                start_head(h)
                with act.Fori(0, NT - 2) as t:
                    step(h, t)
                n = NT * h + NT - 2
                take_pt(n)
                softmax(n + 1)
                take_pt(n + 1)
            start_head(H - 1)
            with act.Fori(0, EARLY) as t:
                step(H - 1, t)
            step(H - 1, EARLY)
            batch_std(0)
            z(0, EARLY // 2)
            n = NT * H - 2
            take_pt(n)
            softmax(n + 1)
            z(EARLY // 2, EARLY)
            take_pt(n + 1)
            for b in (1, 2):
                batch_std(b)
                z(*BATCHES[b])

        @block.vector
        def _(dve):
            def q_lo(t, n):
                dve.wait_ge(qt_hi, n + 1)
                nc.vector.tensor_tensor(qt_r[1][:, :, :], q[:, :, bass.ds(t * P, P)], qt_r[0][:, :, :].bitcast(F32),
                                        ALU.subtract).then_inc(qt_lo, 1)

            def row_max(n):
                dve.wait_ge(share_done, n + 1)
                dve.wait_ge(s_done, n + 2)
                dve.wait_ge(logs_in, 16 * n + 16)
                dve.sem_inc(row_turn, 1)
                nc.vector.tensor_tensor_reduce(sps[:, 0:N], sps[:, 0:N], logs[:, :], 1.0, -BIG / 2, ALU.add, ALU.max,
                                               mx[:, :]).then_inc(mx_done, 1)
                dve.wait_ge(mx_done, n + 1)
                dve.sem_inc(logs_used, 1)
                nc.vector.tensor_scalar(amax[:, :], mx[:, :], r[:, bass.ds(n, 1)], None, ALU.add
                                        ).then_inc(amax_done, 1)
                dve.wait_ge(amax_done, n + 1)
                nc.vector.tensor_tensor(shift[:, :], r[:, bass.ds(n, 1)], amax[:, :], ALU.subtract).then_inc(shift_done, 1)

            def split_g(h, s):
                i = 12 + s
                dve.wait_ge(g_hi, NT * h + s + 1)
                nc.vector.tensor_tensor(g_r[1][:, s, :], wps[i % 2][:, :], g_r[0][:, s, :].bitcast(F32),
                                        ALU.subtract).then_inc(w_free[i % 2], 1)
                if s == NT - 1:
                    dve.wait_ge(w_free[1], use(h, 21) + 2)
                    dve.sem_inc(g_lo, NT)

            def split_pt(n):
                for g, (a, b) in enumerate(TG):
                    dve.wait_ge(pt_hi, 3 * n + g + 1)
                    z = a + len([s for s in range(a, b) if rows_of(s) == P])
                    last = nc.vector.tensor_tensor(pt_r[1][:, a:z, :], tps[g][:, 0:z - a, :],
                                                   pt_r[0][:, a:z, :].bitcast(F32), ALU.subtract)
                    if z < b:
                        last = nc.vector.tensor_tensor(pt_r[1][0:LAST, z, :], tps[g][0:LAST, z - a, :],
                                                       pt_r[0][0:LAST, z, :].bitcast(F32), ALU.subtract)
                    last.then_inc(pt_lo, 1)

            def take_share(t, n):
                dve.wait_ge(exp_done, n + 1)
                nc.vector.tensor_scalar(has[:, bass.ds(t, 1)], den[:, :], 0.0, None, ALU.is_gt)
                nc.vector.tensor_scalar(total[:, :], den[:, :], 2.0 ** -60, None, ALU.max).then_inc(total_done, 1)
                dve.wait_ge(total_done, n + 1)
                nc.vector.reciprocal(share[:, :], total[:, :]).then_inc(share_done, 1)

            def add_head(h, t, n):
                dve.wait_ge(share_done, n + 2)
                dve.wait_ge(w_done[0], use_pv(h, t) + 1)
                yt = y[:, bass.ds(t, 1), :].rearrange("p a d -> p (a d)")
                nc.vector.scalar_tensor_tensor(out=yt, in0=wps[0][:, :], scalar=share[:, :], in1=yt, op0=ALU.mult,
                                               op1=ALU.add).then_inc(w_free[0], 1)

            count = [0]

            def step(ins):
                count[0] += 1
                ins.then_inc(chain, 1)
                dve.wait_ge(chain, count[0])

            dve.sem_inc(pt_lo, 3)
            dve.sem_inc(logs_used, 1)
            dve.sem_inc(share_done, 1)
            w = keep["uw"][:, KT:2 * KT, :]
            step(nc.vector.tensor_copy(w_r[:, :, 0, :], w))
            nc.vector.tensor_tensor(w_r[:, :, 1, :], w, w_r[:, :, 0, :].bitcast(F32), ALU.subtract).then_inc(w_r_done, 1)
            nc.vector.memset(r2[:, :, :], 0.0).then_inc(r2_cleared, 1)

            def h_lo(t):
                dve.wait_ge(ht_hi, t + 1)
                nc.vector.tensor_tensor(h_r[1][:, :, t * P:(t + 1) * P], hps[t % 2][:, :, :],
                                        h_r[0][:, :, t * P:(t + 1) * P].bitcast(F32), ALU.subtract).then_inc(ht_lo, 1)

            h_lo(0)
            h_lo(1)
            for s in range(NT):
                if s == NT - 1:
                    dve.wait_ge(r_done, 1)
                    nc.vector.tensor_copy(probs[0:2 * H, :], sps[0:2 * H, 0:N]).then_inc(r_out, 1)
                dve.wait_ge(w_done[s % 2], s // 2 + 1)
                nc.vector.tensor_tensor(y[:, s, :], wps[s % 2][:, :], keep["s_row"][:, :], ALU.add
                                        ).then_inc(w_free[s % 2], 1)
                if s + 2 < NT:
                    h_lo(s + 2)
            dve.wait_ge(r_turned, 1)
            dve.wait_ge(r2_cleared, 1)
            turned = tps[0][:, 0, 0:2 * H * NT].rearrange("p (t a) -> p t a", t=NT)
            nc.vector.tensor_copy(r2[:, 0:NT - 1, :], turned[:, 0:NT - 1, :])
            step(nc.vector.tensor_copy(r2[0:LAST, NT - 1, :], turned[0:LAST, NT - 1, :]))
            step(nc.vector.tensor_tensor(r3[:, :, :], r2[:, :, 0:H], r2[:, :, H:2 * H], ALU.add))
            for h in range(H):
                last = nc.vector.tensor_scalar(r[:, h * NT:(h + 1) * NT], r3[:, :, h], keep["bqbk"][:, h:h + 1],
                                               SCALE, ALU.add, ALU.mult)
            last.then_inc(r_ready, 1)
            dve.wait_ge(r_ready, 1)

            def start_head(h):
                q_lo(0, NT * h)
                for s in range(NT // 2):
                    split_g(h, s)
                row_max(NT * h)
                q_lo(1, NT * h + 1)
                for s in range(NT // 2, NT):
                    split_g(h, s)

            def tile_stats(t):
                dve.wait_ge(w_free[0], use_pv(H - 1, t) + 2)
                yt = y[:, bass.ds(t, 1), :].rearrange("p a d -> p (a d)")
                nc.vector.scalar_tensor_tensor(out=yt, in0=keep["v_row"][:, :], scalar=has[:, bass.ds(t, 1)], in1=yt,
                                               op0=ALU.mult, op1=ALU.add).then_inc(yb_done, 1)
                dve.wait_ge(yb_done, t + 1)
                nc.vector.bn_stats(stats[:, bass.ds(t, 1), :].rearrange("p a b -> p (a b)"), yt).then_inc(st_done, 1)

            def batch_var(b):
                start, end = BATCHES[b]
                dve.wait_ge(st_done, end)
                for t in range(start, end):
                    last = nc.vector.bn_aggr(mv[:, t, :], stats[:, t, :])
                step(last)
                nc.vector.tensor_scalar(std[:, start:end], mv[:, start:end, 1], EPS, None, ALU.add).then_inc(var_done, 1)

            def batch_norm(b):
                start, end = BATCHES[b]
                dve.wait_ge(std_done, b + 1)
                step(nc.vector.reciprocal(rstd[:, start:end], std[:, start:end]))
                nc.vector.scalar_tensor_tensor(out=nmr[:, start:end], in0=mv[:, start:end, 0], scalar=-1.0,
                                               in1=rstd[:, start:end], op0=ALU.mult, op1=ALU.mult).then_inc(norm_ready, 1)

            def times_gamma(t):
                p = rows_of(t)
                dve.wait_ge(z_done, t + 1)
                nc.vector.tensor_tensor(y[0:p, t, :], y[0:p, t, :], gamma[0:p, :], ALU.mult).then_inc(zg_done, 1)

            def finish(t):
                times_gamma(t)
                dve.wait_ge(zg_done, t + 1)
                dve.wait_ge(xb_done, t + 1)
                p = rows_of(t)
                nc.vector.tensor_tensor(y[0:p, t, :], y[0:p, t, :], x[0:p, t, :], ALU.add).then_inc(out_late, 1)

            with dve.Fori(0, H - 1) as h:
                start_head(h)
                with dve.Fori(0, NT - 2) as t:
                    n = NT * h + t
                    take_share(t, n)
                    split_pt(n)
                    row_max(n + 1)
                    q_lo(t + 2, n + 2)
                    add_head(h, t, n)
                n = NT * h + NT - 2
                take_share(NT - 2, n)
                split_pt(n)
                row_max(n + 1)
                add_head(h, NT - 2, n)
                take_share(NT - 1, n + 1)
                split_pt(n + 1)
                add_head(h, NT - 1, n + 1)
            h = H - 1
            start_head(h)
            with dve.Fori(0, EARLY) as t:
                n = NT * h + t
                take_share(t, n)
                split_pt(n)
                row_max(n + 1)
                q_lo(t + 2, n + 2)
                add_head(h, t, n)
                tile_stats(t)
            dve.wait_ge(row_in, 32)
            n = NT * h + EARLY
            take_share(EARLY, n)
            split_pt(n)
            batch_var(0)
            row_max(n + 1)
            q_lo(EARLY + 2, n + 2)
            batch_norm(0)
            add_head(h, EARLY, n)
            tile_stats(EARLY)
            take_share(NT - 2, n + 1)
            split_pt(n + 1)
            row_max(n + 2)
            for t in range(EARLY // 2):
                times_gamma(t)
            add_head(h, NT - 2, n + 1)
            tile_stats(NT - 2)
            take_share(NT - 1, n + 2)
            split_pt(n + 2)
            batch_var(1)
            for t in range(EARLY // 2, EARLY):
                times_gamma(t)
            batch_norm(1)
            for t in range(*BATCHES[1]):
                finish(t)
            add_head(h, NT - 1, n + 2)
            tile_stats(NT - 1)
            batch_var(2)
            batch_norm(2)
            finish(NT - 1)


def build(nc, io):
    with ExitStack() as ctx:
        keep_sb = lambda name, shape, dt: ctx.enter_context(nc.sbuf_tensor(name, shape, dt))
        sem = lambda name: ctx.enter_context(nc.semaphore(name))
        keep = {
            "h": keep_sb("h", [P, NT, D], F32),
            "m_hi": keep_sb("m_hi", [P, KT, D], F32R),
            "m_lo": keep_sb("m_lo", [P, KT, D], F32R),
            "a_hi": keep_sb("a_hi", [P, KT, D], F32R),
            "a_lo": keep_sb("a_lo", [P, KT, D], F32R),
            "ident": keep_sb("ident", [P, P], F32),
            "uw": keep_sb("uw", [P, 2 * KT, H], F32),
            "bqbk": keep_sb("bqbk", [P, H], F32),
            "v_row": keep_sb("v_row", [P, D], F32),
            "s_row": keep_sb("s_row", [P, D], F32),
        }
        r32 = lambda name, shape: nc.dram_tensor(name, shape, F32).ap()
        dram = {
            "M": r32("M_parts", [H, 2, P, KT, D]),
            "A": r32("A_parts", [H, 2, P, KT, D]),
            "L": nc.dram_tensor("log_counts", [NT, P, N], F32).ap(),
        }
        with ExitStack() as sems:
            fold_and_count(nc, io, keep, dram, lambda name: sems.enter_context(nc.semaphore(name)))
        attend(nc, io, keep, dram, sem)


def kernel(x, src, dst, L0_gnn_Wq, L0_gnn_bq, L0_gnn_Wk, L0_gnn_bk, L0_gnn_Wv, L0_gnn_bv, L0_gnn_Wskip, L0_gnn_bskip,
           L0_gnn_Wlin, L0_gnn_blin, L0_gnn_gamma, L0_gnn_beta):
    import numpy as np
    import concourse.bacc as bacc
    from concourse.bass_utils import run_bass_kernel_spmd

    tiled = lambda w: np.ascontiguousarray(np.asarray(w).reshape(H, KT, P, D).transpose(0, 2, 1, 3))
    edges = lambda e: np.ascontiguousarray(np.asarray(e).reshape(CH, EP).T)
    column = lambda b: np.ascontiguousarray(np.asarray(b).reshape(H * KT, P).T)
    arrays = {
        "x": np.ascontiguousarray(x), "src": edges(src), "dst": edges(dst),
        "Wq": tiled(np.asarray(L0_gnn_Wq).T), "Wk": tiled(np.asarray(L0_gnn_Wk).T),
        "Wv": tiled(np.asarray(L0_gnn_Wv).T), "Ws": tiled(np.asarray(L0_gnn_Wskip).T), "Wl": tiled(L0_gnn_Wlin),
        "bq": column(L0_gnn_bq), "bk": column(L0_gnn_bk), "bv": column(L0_gnn_bv), "bs": column(L0_gnn_bskip),
        "blin": np.ascontiguousarray(L0_gnn_blin), "gamma": np.ascontiguousarray(L0_gnn_gamma),
        "beta": np.ascontiguousarray(L0_gnn_beta),
    }
    nc = bacc.Bacc("TRN2", target_bir_lowering=False, num_devices=1)
    io = {name: nc.dram_tensor(f"in_{name}", a.shape, mybir.dt.from_np(a.dtype), kind="ExternalInput").ap()
          for name, a in arrays.items()}
    io["out"] = nc.dram_tensor("out", (N, D), F32, kind="ExternalOutput").ap()
    build(nc, io)
    result = run_bass_kernel_spmd(nc, [{f"in_{name}": a for name, a in arrays.items()}], core_ids=[0])
    return result.results[0]["out"]
```
